# Optimizing a Trainium2 kernel written in Bass

```python
import numpy as np
import jax
import jax.numpy as jnp

def _softmax(x, axis=-1):
    return jax.nn.softmax(x, axis=axis)

def _gelu(x):
    return jax.nn.gelu(x, approximate=True)

def _silu(x):
    return jax.nn.silu(x)

def _sigmoid(x):
    return jax.nn.sigmoid(x)

def _layernorm(x, axis=-1, eps=1e-05):
    m = jnp.mean(x, axis=axis, keepdims=True)
    v = jnp.var(x, axis=axis, keepdims=True)
    return (x - m) / jnp.sqrt(v + eps)

def _scatter_add(tgt, idx, src, axis=0):
    return tgt.at[idx].add(src)

def _segment_sum(src, seg, n):
    return jax.ops.segment_sum(src, seg, n)
kernel_name = 'mk_seq_postln_d4_jaxref_r8_435d60'

def setup_inputs(seed: int=0):
    np.random.seed(seed)
    _w = jnp.asarray

    def _L0_attn_setup():
        import jax, jax.numpy as jnp
        import numpy as np
        MODEL_DIM = 128
        HEADS = 16
        HEAD_DIM = MODEL_DIM // HEADS
        B, T = (2, 256)
        TB_LEN = 500
        key = jax.random.key(seed)
        ks = jax.random.split(key, 12)
        s = 0.02
        d = MODEL_DIM
        return {'x': jax.random.normal(ks[0], (B, T, d), dtype=jnp.float32), 'Wq': jax.random.normal(ks[1], (d, d), dtype=jnp.float32) * s, 'bq': jnp.zeros((d,), jnp.float32), 'Wk': jax.random.normal(ks[2], (d, d), dtype=jnp.float32) * s, 'bk': jnp.zeros((d,), jnp.float32), 'Wv': jax.random.normal(ks[3], (d, d), dtype=jnp.float32) * s, 'bv': jnp.zeros((d,), jnp.float32), 'Wo': jax.random.normal(ks[4], (d, d), dtype=jnp.float32) * s, 'bo': jnp.zeros((d,), jnp.float32), 'et_gate': jax.random.normal(ks[5], (1, 1, 1), dtype=jnp.float32), 'is_gate': jax.random.normal(ks[6], (1, 1, 1), dtype=jnp.float32), 'time_bias': jnp.linspace(-1.0, 1.0, TB_LEN, dtype=jnp.float32).reshape(1, 1, TB_LEN)}
    _L0_attn_in = _L0_attn_setup()

    def _L0_ffn_setup():
        import jax, jax.numpy as jnp
        import numpy as np

        def _binarize(w):
            alpha = jax.lax.stop_gradient(jnp.mean(jnp.abs(w), axis=1, keepdims=True))
            bw = alpha * jnp.sign(w)
            return w + jax.lax.stop_gradient(bw - w)
        key = jax.random.key(seed)
        k1, k2, k3, k4, k5 = jax.random.split(key, 5)
        D, H = (128, 512)
        x = jax.random.normal(k1, (64, 196, D), dtype=jnp.float32)
        w1 = jax.random.normal(k2, (H, D), dtype=jnp.float32) * 0.02
        b1 = jax.random.normal(k3, (H,), dtype=jnp.float32) * 0.02
        w2 = jax.random.normal(k4, (D, H), dtype=jnp.float32) * 0.02
        b2 = jax.random.normal(k5, (D,), dtype=jnp.float32) * 0.02
        return {'x': x, 'w1': w1, 'b1': b1, 'w2': w2, 'b2': b2}
    _L0_ffn_in = _L0_ffn_setup()

    def _L1_attn_setup():
        import jax, jax.numpy as jnp
        import numpy as np
        NUM_HEADS = 16
        EPS = 1e-06

        def _phi(x):
            return jax.nn.elu(x) + 1.0
        key = jax.random.key(seed)
        ks = jax.random.split(key, 5)
        B, L, D = (4, 1024, 128)
        scale = 0.02
        return {'x': jax.random.normal(ks[0], (B, L, D), dtype=jnp.float32), 'Wq': jax.random.normal(ks[1], (D, D), dtype=jnp.float32) * scale, 'Wk': jax.random.normal(ks[2], (D, D), dtype=jnp.float32) * scale, 'Wv': jax.random.normal(ks[3], (D, D), dtype=jnp.float32) * scale, 'Wo': jax.random.normal(ks[4], (D, D), dtype=jnp.float32) * scale}
    _L1_attn_in = _L1_attn_setup()

    def _L1_ffn_setup():
        import jax, jax.numpy as jnp
        import numpy as np
        N, T, D = (4, 512, 128)
        NUM_EXPERTS = 8
        EXPERT_CAP = 2.0
        MLP_RATIO = 4
        HIDDEN = MLP_RATIO * D
        key = jax.random.key(seed)
        k1, k2, k3, k4 = jax.random.split(key, 4)
        x = jax.random.normal(k1, (N, T, D), dtype=jnp.float32)
        gate_w = jax.random.truncated_normal(k2, -2.0, 2.0, (D, NUM_EXPERTS), dtype=jnp.float32) * 0.02
        w1 = jax.random.normal(k3, (NUM_EXPERTS, D, HIDDEN), dtype=jnp.float32) * 0.02
        w2 = jax.random.normal(k4, (NUM_EXPERTS, HIDDEN, D), dtype=jnp.float32) * 0.02
        return {'x': x, 'gate_w': gate_w, 'w1': w1, 'w2': w2}
    _L1_ffn_in = _L1_ffn_setup()

    def _L2_attn_setup():
        import math
        import jax, jax.numpy as jnp
        import numpy as np
        M_WIN = 64
        P = 8
        L_LEV = 4
        N_HEAD = 16

        def _pool(x, s):
            bh, n, d = x.shape
            return x.reshape(bh, n // s, s, d).mean(axis=2)

        def _shift_prev(xb):
            return jnp.pad(xb, ((0, 0), (1, 0), (0, 0), (0, 0)))[:, :-1]

        def _mla(q, k, v, m, p, L, scale_attn=True):
            bh, n, d = q.shape
            q = q / math.sqrt(d)
            Kls, Vls = ([k], [v])
            for l in range(L):
                s = m * 2 ** l // p
                Kls.append(_pool(k, s))
                Vls.append(_pool(v, s))
            nb = n // m
            Qc = q.reshape(bh, nb, m, d)
            Kc = k.reshape(bh, nb, m, d)
            Kwin = jnp.concatenate([_shift_prev(Kc), Kc], axis=2)
            S = jnp.einsum('bcqd,bckd->bcqk', Qc, Kwin)
            qg = jnp.broadcast_to(jnp.arange(m)[:, None], (m, m))
            kg = jnp.arange(m)[:, None] + 1 + jnp.arange(m)[None, :]
            As = [S[:, :, qg, kg].reshape(bh, n, m)]
            for l in range(1, L + 1):
                w = m * 2 ** (l - 1)
                nbl = n // w
                Kprev = _shift_prev(Kls[l].reshape(bh, nbl, p, d))
                Al = jnp.einsum('bcwd,bcpd->bcwp', q.reshape(bh, nbl, w, d), Kprev)
                As.append(Al.reshape(bh, n, p))
            maxes = jnp.stack([A.max(axis=-1) for A in As], axis=-1)
            mn = maxes.min(axis=-1, keepdims=True)
            exps = [jnp.exp(A - mn) for A in As]
            scales = [1] + [m * 2 ** (l - 1) // p for l in range(1, L + 1)]
            esum = exps[0].sum(axis=-1)
            for l in range(1, L + 1):
                s_l = exps[l].sum(axis=-1)
                esum = esum + (s_l * scales[l] if scale_attn else s_l)
            esum = esum[..., None]
            Cs = [(scales[l] if l > 0 and scale_attn else 1) * exps[l] / esum for l in range(L + 1)]
            C0 = Cs[0].reshape(bh, nb, m, m)
            Cfull = jnp.zeros((bh, nb, m, 2 * m), C0.dtype).at[:, :, qg, kg].set(C0)
            Vc = v.reshape(bh, nb, m, d)
            Vwin = jnp.concatenate([_shift_prev(Vc), Vc], axis=2)
            out = jnp.einsum('bcqk,bckd->bcqd', Cfull, Vwin).reshape(bh, n, d)
            for l in range(1, L + 1):
                w = m * 2 ** (l - 1)
                nbl = n // w
                Vprev = _shift_prev(Vls[l].reshape(bh, nbl, p, d))
                out = out + jnp.einsum('bcwp,bcpd->bcwd', Cs[l].reshape(bh, nbl, w, p), Vprev).reshape(bh, n, d)
            return out
        key = jax.random.key(seed)
        ks = jax.random.split(key, 4)
        B, T, C = (8, 256, 128)
        x = jax.random.normal(ks[0], (B, T, C), jnp.float32)
        W_attn = jax.random.normal(ks[1], (C, 3 * C), jnp.float32) * 0.02
        b_attn = jnp.zeros((3 * C,), jnp.float32)
        W_proj = jax.random.normal(ks[2], (C, C), jnp.float32) * 0.02
        b_proj = jnp.zeros((C,), jnp.float32)
        return {'x': x, 'W_attn': W_attn, 'b_attn': b_attn, 'W_proj': W_proj, 'b_proj': b_proj}
    _L2_attn_in = _L2_attn_setup()

    def _L2_ffn_setup():
        import jax, jax.numpy as jnp
        import numpy as np
        ALPHA = 1.0
        key = jax.random.key(seed)
        ks = jax.random.split(key, 7)
        B, S, IN, OUT = (8, 1024, 128, 128)
        RANK, DDIM, UDIM = (4, 100, 50)
        return {'hidden_states': jax.random.normal(ks[0], (B, S, IN), dtype=jnp.float32), 'W': jax.random.normal(ks[1], (OUT, IN), dtype=jnp.float32) * 0.02, 'b': jax.random.normal(ks[2], (OUT,), dtype=jnp.float32) * 0.02, 'lora_down': jax.random.normal(ks[3], (RANK, DDIM), dtype=jnp.float32) * 0.1, 'lora_up': jax.random.normal(ks[4], (UDIM, RANK), dtype=jnp.float32) * 0.1, 'down_aux': jax.random.normal(ks[5], (DDIM, IN), dtype=jnp.float32) * 0.03, 'up_aux': jax.random.normal(ks[6], (OUT, UDIM), dtype=jnp.float32) * 0.03}
    _L2_ffn_in = _L2_ffn_setup()

    def _L3_attn_setup():
        import jax, jax.numpy as jnp
        import numpy as np
        B, N, D = (4, 256, 128)
        H = 8
        DK = D // H
        DV = D // H
        DF = 2 * DK
        CHUNK = 64
        RMS_EPS = 1e-05

        def _hedgehog(x, w, b):
            y = jnp.einsum('bhnd,ed->bhne', x, w) + b
            return jnp.concatenate([jnp.exp(y), jnp.exp(-y)], axis=-1)

        def _fused_chunk_linear_attn(q, k, v):
            b, h, n, df = q.shape
            dv = v.shape[-1]
            nc = n // CHUNK

            def to_chunks(t):
                d = t.shape[-1]
                return t.reshape(b, h, nc, CHUNK, d).transpose(2, 0, 1, 3, 4)
            qc, kc, vc = (to_chunks(q), to_chunks(k), to_chunks(v))
            mask = jnp.tril(jnp.ones((CHUNK, CHUNK), dtype=bool))

            def step(S, inp):
                qi, ki, vi = inp
                attn = jnp.einsum('bhcd,bhed->bhce', qi, ki)
                attn = jnp.where(mask, attn, 0.0)
                intra = jnp.einsum('bhce,bhev->bhcv', attn, vi)
                inter = jnp.einsum('bhcd,bhdv->bhcv', qi, S)
                S = S + jnp.einsum('bhcd,bhcv->bhdv', ki, vi)
                return (S, intra + inter)
            S0 = jnp.zeros((b, h, df, dv), dtype=q.dtype)
            _, oc = jax.lax.scan(step, S0, (qc, kc, vc))
            return oc.transpose(1, 2, 0, 3, 4).reshape(b, h, n, dv)
        key = jax.random.key(seed)
        ks = jax.random.split(key, 10)
        s = D ** (-0.5)
        x = jax.random.normal(ks[0], (B, N, D), dtype=jnp.float32)
        Wq = jax.random.normal(ks[1], (D, D), dtype=jnp.float32) * s
        Wk = jax.random.normal(ks[2], (D, D), dtype=jnp.float32) * s
        Wv = jax.random.normal(ks[3], (D, D), dtype=jnp.float32) * s
        Wo = jax.random.normal(ks[4], (D, D), dtype=jnp.float32) * s
        eye = jnp.eye(DK, dtype=jnp.float32)
        fmq_w = eye + 0.02 * jax.random.normal(ks[5], (DK, DK), dtype=jnp.float32)
        fmq_b = 0.02 * jax.random.normal(ks[6], (DK,), dtype=jnp.float32)
        fmk_w = eye + 0.02 * jax.random.normal(ks[7], (DK, DK), dtype=jnp.float32)
        fmk_b = 0.02 * jax.random.normal(ks[8], (DK,), dtype=jnp.float32)
        rms_w = 1.0 + 0.1 * jax.random.normal(ks[9], (DV,), dtype=jnp.float32)
        return {'x': x, 'Wq': Wq, 'Wk': Wk, 'Wv': Wv, 'Wo': Wo, 'fmq_w': fmq_w, 'fmq_b': fmq_b, 'fmk_w': fmk_w, 'fmk_b': fmk_b, 'rms_w': rms_w}
    _L3_attn_in = _L3_attn_setup()

    def _L3_ffn_setup():
        import jax, jax.numpy as jnp
        import numpy as np
        DIM = 128
        DEPTH = 6
        HEADS = 16
        DIM_HEAD = 64
        WINDOW = 32
        INNER = HEADS * DIM_HEAD
        DIM_INNER = int(DIM * 4 * 2 / 3)
        QK_SCALE = 8.0

        def shift_tokens(t):
            a, s = jnp.split(t, 2, -1)
            s = jnp.pad(s, ((0, 0), (1, 0), (0, 0)))[:, :-1]
            return jnp.concatenate([a, s], -1)

        def l2norm(t):
            return t / jnp.maximum(jnp.linalg.norm(t, axis=-1, keepdims=True), 1e-12)

        def rotate_half(x):
            x1, x2 = jnp.split(x, 2, -1)
            return jnp.concatenate([-x2, x1], -1)

        def rotary_tables(n):
            half = jnp.arange(0, DIM_HEAD, 2, dtype=jnp.float32)
            inv_freq = 1.0 / 10000.0 ** (half / DIM_HEAD)
            t = jnp.arange(n, dtype=jnp.float32)
            freqs = t[:, None] * inv_freq[None, :]
            freqs = jnp.concatenate([freqs, freqs], -1)
            base_scale = (half + 0.4 * DIM_HEAD) / (1.4 * DIM_HEAD)
            power = (t - n // 2) / (WINDOW // 2)
            scale = base_scale[None, :] ** power[:, None]
            scale = jnp.concatenate([scale, scale], -1)
            return (freqs, scale)

        def local_attention(q, k, v):
            b, h, n, d = q.shape
            w = WINDOW
            nw = n // w
            bq = q.reshape(b, h, nw, w, d)
            bk = k.reshape(b, h, nw, w, d)
            bv = v.reshape(b, h, nw, w, d)

            def look(t):
                p = jnp.pad(t, ((0, 0), (0, 0), (1, 0), (0, 0), (0, 0)))
                return jnp.concatenate([p[:, :, :nw], p[:, :, 1:]], axis=3)
            bk2, bv2 = (look(bk), look(bv))
            seq = jnp.arange(n).reshape(nw, w)
            seq_p = jnp.pad(seq, ((1, 0), (0, 0)), constant_values=-1)
            jt = jnp.concatenate([seq_p[:nw], seq_p[1:]], axis=1)
            it = seq[:, :, None]
            jb = jt[:, None, :]
            mask = (it < jb) | (it > jb + w) | (jb == -1)
            sim = jnp.einsum('bhwie,bhwje->bhwij', bq, bk2) * QK_SCALE
            sim = jnp.where(mask, -jnp.finfo(sim.dtype).max, sim)
            attn = jax.nn.softmax(sim, -1)
            out = jnp.einsum('bhwij,bhwje->bhwie', attn, bv2)
            return out.reshape(b, h, n, d)

        def attn_layer(x, Wqkv, qs, ksc, Wo):
            b, n, _ = x.shape
            qkv = x @ Wqkv
            q, k, v = jnp.split(qkv, 3, -1)
            sh = lambda t: t.reshape(b, n, HEADS, DIM_HEAD).transpose(0, 2, 1, 3)
            q, k, v = (sh(q), sh(k), sh(v))
            q = l2norm(q) * qs
            k = l2norm(k) * ksc
            freqs, scale = rotary_tables(n)
            cos, sin = (jnp.cos(freqs), jnp.sin(freqs))
            q = q * cos * scale + rotate_half(q) * sin * scale
            inv = 1.0 / scale
            k = k * cos * inv + rotate_half(k) * sin * inv
            out = local_attention(q, k, v)
            out = out.transpose(0, 2, 1, 3).reshape(b, n, INNER)
            return out @ Wo

        def ffn_layer(x, g, bln, W1, b1, W2, b2):
            mu = x.mean(-1, keepdims=True)
            var = ((x - mu) ** 2).mean(-1, keepdims=True)
            xn = (x - mu) / jnp.sqrt(var + 1e-05) * g + bln
            hg = xn @ W1 + b1
            a, gate = jnp.split(hg, 2, -1)
            return a * jax.nn.gelu(gate, approximate=False) @ W2 + b2
        key = jax.random.key(seed)
        ks = jax.random.split(key, 8)
        B, N = (2, 256)
        init = lambda k, shape: jax.random.normal(k, shape, jnp.float32) * 0.02
        return {'x': jax.random.normal(ks[0], (B, N, DIM), jnp.float32), 'Wqkv': init(ks[1], (DEPTH, DIM, 3 * INNER)), 'q_scale': jnp.ones((DEPTH, DIM_HEAD), jnp.float32), 'k_scale': jnp.ones((DEPTH, DIM_HEAD), jnp.float32), 'Wo': init(ks[2], (DEPTH, INNER, DIM)), 'ln_g': jnp.ones((DEPTH, DIM), jnp.float32), 'ln_b': jnp.zeros((DEPTH, DIM), jnp.float32), 'W1': init(ks[3], (DEPTH, DIM, 2 * DIM_INNER)), 'b1': jnp.zeros((DEPTH, 2 * DIM_INNER), jnp.float32), 'W2': init(ks[4], (DEPTH, DIM_INNER, DIM)), 'b2': jnp.zeros((DEPTH, DIM), jnp.float32)}
    _L3_ffn_in = _L3_ffn_setup()
    _d = {'L0_attn_x': _L0_attn_in['x'], 'L0_attn_Wq': _L0_attn_in['Wq'], 'L0_attn_bq': _L0_attn_in['bq'], 'L0_attn_Wk': _L0_attn_in['Wk'], 'L0_attn_bk': _L0_attn_in['bk'], 'L0_attn_Wv': _L0_attn_in['Wv'], 'L0_attn_bv': _L0_attn_in['bv'], 'L0_attn_Wo': _L0_attn_in['Wo'], 'L0_attn_bo': _L0_attn_in['bo'], 'L0_attn_et_gate': _L0_attn_in['et_gate'], 'L0_attn_is_gate': _L0_attn_in['is_gate'], 'L0_attn_time_bias': _L0_attn_in['time_bias'], 'L0_ffn_w1': _L0_ffn_in['w1'], 'L0_ffn_b1': _L0_ffn_in['b1'], 'L0_ffn_w2': _L0_ffn_in['w2'], 'L0_ffn_b2': _L0_ffn_in['b2'], 'L1_attn_Wq': _L1_attn_in['Wq'], 'L1_attn_Wk': _L1_attn_in['Wk'], 'L1_attn_Wv': _L1_attn_in['Wv'], 'L1_attn_Wo': _L1_attn_in['Wo'], 'L1_ffn_gate_w': _L1_ffn_in['gate_w'], 'L1_ffn_w1': _L1_ffn_in['w1'], 'L1_ffn_w2': _L1_ffn_in['w2'], 'L2_attn_W_attn': _L2_attn_in['W_attn'], 'L2_attn_b_attn': _L2_attn_in['b_attn'], 'L2_attn_W_proj': _L2_attn_in['W_proj'], 'L2_attn_b_proj': _L2_attn_in['b_proj'], 'L2_ffn_W': _L2_ffn_in['W'], 'L2_ffn_b': _L2_ffn_in['b'], 'L2_ffn_lora_down': _L2_ffn_in['lora_down'], 'L2_ffn_lora_up': _L2_ffn_in['lora_up'], 'L2_ffn_down_aux': _L2_ffn_in['down_aux'], 'L2_ffn_up_aux': _L2_ffn_in['up_aux'], 'L3_attn_Wq': _L3_attn_in['Wq'], 'L3_attn_Wk': _L3_attn_in['Wk'], 'L3_attn_Wv': _L3_attn_in['Wv'], 'L3_attn_Wo': _L3_attn_in['Wo'], 'L3_attn_fmq_w': _L3_attn_in['fmq_w'], 'L3_attn_fmq_b': _L3_attn_in['fmq_b'], 'L3_attn_fmk_w': _L3_attn_in['fmk_w'], 'L3_attn_fmk_b': _L3_attn_in['fmk_b'], 'L3_attn_rms_w': _L3_attn_in['rms_w'], 'L3_ffn_Wqkv': _L3_ffn_in['Wqkv'], 'L3_ffn_q_scale': _L3_ffn_in['q_scale'], 'L3_ffn_k_scale': _L3_ffn_in['k_scale'], 'L3_ffn_Wo': _L3_ffn_in['Wo'], 'L3_ffn_ln_g': _L3_ffn_in['ln_g'], 'L3_ffn_ln_b': _L3_ffn_in['ln_b'], 'L3_ffn_W1': _L3_ffn_in['W1'], 'L3_ffn_b1': _L3_ffn_in['b1'], 'L3_ffn_W2': _L3_ffn_in['W2'], 'L3_ffn_b2': _L3_ffn_in['b2']}
    _x0 = _d['L0_attn_x']
    _d['L0_attn_x'] = jax.random.normal(jax.random.fold_in(jax.random.key(seed), 1), (4, 1024, 128), dtype=_x0.dtype)
    del _x0
    return _d

def reference(L0_attn_x, L0_attn_Wq, L0_attn_bq, L0_attn_Wk, L0_attn_bk, L0_attn_Wv, L0_attn_bv, L0_attn_Wo, L0_attn_bo, L0_attn_et_gate, L0_attn_is_gate, L0_attn_time_bias, L0_ffn_w1, L0_ffn_b1, L0_ffn_w2, L0_ffn_b2, L1_attn_Wq, L1_attn_Wk, L1_attn_Wv, L1_attn_Wo, L1_ffn_gate_w, L1_ffn_w1, L1_ffn_w2, L2_attn_W_attn, L2_attn_b_attn, L2_attn_W_proj, L2_attn_b_proj, L2_ffn_W, L2_ffn_b, L2_ffn_lora_down, L2_ffn_lora_up, L2_ffn_down_aux, L2_ffn_up_aux, L3_attn_Wq, L3_attn_Wk, L3_attn_Wv, L3_attn_Wo, L3_attn_fmq_w, L3_attn_fmq_b, L3_attn_fmk_w, L3_attn_fmk_b, L3_attn_rms_w, L3_ffn_Wqkv, L3_ffn_q_scale, L3_ffn_k_scale, L3_ffn_Wo, L3_ffn_ln_g, L3_ffn_ln_b, L3_ffn_W1, L3_ffn_b1, L3_ffn_W2, L3_ffn_b2):

    def _L0_attn_ref(x, Wq, bq, Wk, bk, Wv, bv, Wo, bo, et_gate, is_gate, time_bias):
        import jax, jax.numpy as jnp
        import numpy as np
        MODEL_DIM = 128
        HEADS = 16
        HEAD_DIM = MODEL_DIM // HEADS
        B, T = (2, 256)
        TB_LEN = 500
        Bb, Tt, D = x.shape
        H, hd = (HEADS, HEAD_DIM)
        Q = (x @ Wq.T + bq).reshape(Bb, Tt, H, hd).transpose(0, 2, 1, 3)
        K = (x @ Wk.T + bk).reshape(Bb, Tt, H, hd).transpose(0, 2, 1, 3)
        V = (x @ Wv.T + bv).reshape(Bb, Tt, H, hd).transpose(0, 2, 1, 3)
        scores = jnp.einsum('bhqd,bhkd->bhqk', Q, K) / jnp.sqrt(jnp.float32(hd))
        pos = jnp.arange(Tt)[None, :] - jnp.arange(Tt)[:, None]
        idx = jnp.clip(pos + TB_LEN // 2, 0, TB_LEN - 1)
        tp = time_bias[:, :, idx]
        tp = jnp.squeeze(tp, axis=1)[None, None]
        scores = scores + jax.nn.sigmoid(et_gate) * tp + is_gate
        attn = jax.nn.softmax(scores, axis=-1)
        context = jnp.matmul(attn, V)
        context = context.transpose(0, 2, 1, 3, 4).reshape(Bb, Tt, D)
        return context @ Wo.T + bo

    def _L0_ffn_ref(x, w1, b1, w2, b2):
        import jax, jax.numpy as jnp
        import numpy as np

        def _binarize(w):
            alpha = jax.lax.stop_gradient(jnp.mean(jnp.abs(w), axis=1, keepdims=True))
            bw = alpha * jnp.sign(w)
            return w + jax.lax.stop_gradient(bw - w)
        bw1 = _binarize(w1)
        h = jnp.einsum('bsd,hd->bsh', x, bw1) + b1
        h = jax.nn.gelu(h, approximate=False)
        bw2 = _binarize(w2)
        out = jnp.einsum('bsh,dh->bsd', h, bw2) + b2
        return out

    def _L1_attn_ref(x, Wq, Wk, Wv, Wo):
        import jax, jax.numpy as jnp
        import numpy as np
        NUM_HEADS = 16
        EPS = 1e-06

        def _phi(x):
            return jax.nn.elu(x) + 1.0
        B, L, D = x.shape
        H = NUM_HEADS
        dh = D // H
        Q = x @ Wq
        K = x @ Wk
        V = x @ Wv
        Qh = Q.reshape(B, L, H, dh).transpose(0, 2, 1, 3)
        Kh = K.reshape(B, L, H, dh).transpose(0, 2, 1, 3)
        Vh = V.reshape(B, L, H, dh).transpose(0, 2, 1, 3)
        Qf = _phi(Qh)
        Kf = _phi(Kh)
        Kv = jnp.einsum('bhlm,bhln->bhmn', Kf, Vh)
        K1 = jnp.sum(Kf, axis=2)
        num = jnp.einsum('bhlm,bhmn->bhln', Qf, Kv)
        den = jnp.einsum('bhlm,bhm->bhl', Qf, K1) + EPS
        out = num / den[..., None]
        out = out.transpose(0, 2, 1, 3).reshape(B, L, D)
        return out @ Wo

    def _L1_ffn_ref(x, gate_w, w1, w2):
        import jax, jax.numpy as jnp
        import numpy as np
        N, T, D = (4, 512, 128)
        NUM_EXPERTS = 8
        EXPERT_CAP = 2.0
        MLP_RATIO = 4
        HIDDEN = MLP_RATIO * D
        x = x.astype(jnp.float32)
        n, t, d = x.shape
        k = int(EXPERT_CAP * t / NUM_EXPERTS)
        scores = jnp.einsum('ntd,de->nte', x, gate_w)
        probs = jax.nn.softmax(scores, axis=-1)
        probs = jnp.transpose(probs, (0, 2, 1))
        g, m = jax.lax.top_k(probs, k)
        xin = jax.vmap(lambda xb, mb: xb[mb])(x, m)
        h = jax.nn.gelu(jnp.einsum('nekd,edf->nekf', xin, w1))
        h = jnp.einsum('nekf,efd->nekd', h, w2)
        weighted = g[..., None] * h
        flat_idx = (m + jnp.arange(n, dtype=m.dtype)[:, None, None] * t).reshape(-1)
        out = jnp.zeros((n * t, d), dtype=jnp.float32).at[flat_idx].add(weighted.reshape(-1, d))
        out = out.reshape(n, t, d)
        return out.astype(jnp.bfloat16)

    def _L2_attn_ref(x, W_attn, b_attn, W_proj, b_proj):
        import math
        import jax, jax.numpy as jnp
        import numpy as np
        M_WIN = 64
        P = 8
        L_LEV = 4
        N_HEAD = 16

        def _pool(x, s):
            bh, n, d = x.shape
            return x.reshape(bh, n // s, s, d).mean(axis=2)

        def _shift_prev(xb):
            return jnp.pad(xb, ((0, 0), (1, 0), (0, 0), (0, 0)))[:, :-1]

        def _mla(q, k, v, m, p, L, scale_attn=True):
            bh, n, d = q.shape
            q = q / math.sqrt(d)
            Kls, Vls = ([k], [v])
            for l in range(L):
                s = m * 2 ** l // p
                Kls.append(_pool(k, s))
                Vls.append(_pool(v, s))
            nb = n // m
            Qc = q.reshape(bh, nb, m, d)
            Kc = k.reshape(bh, nb, m, d)
            Kwin = jnp.concatenate([_shift_prev(Kc), Kc], axis=2)
            S = jnp.einsum('bcqd,bckd->bcqk', Qc, Kwin)
            qg = jnp.broadcast_to(jnp.arange(m)[:, None], (m, m))
            kg = jnp.arange(m)[:, None] + 1 + jnp.arange(m)[None, :]
            As = [S[:, :, qg, kg].reshape(bh, n, m)]
            for l in range(1, L + 1):
                w = m * 2 ** (l - 1)
                nbl = n // w
                Kprev = _shift_prev(Kls[l].reshape(bh, nbl, p, d))
                Al = jnp.einsum('bcwd,bcpd->bcwp', q.reshape(bh, nbl, w, d), Kprev)
                As.append(Al.reshape(bh, n, p))
            maxes = jnp.stack([A.max(axis=-1) for A in As], axis=-1)
            mn = maxes.min(axis=-1, keepdims=True)
            exps = [jnp.exp(A - mn) for A in As]
            scales = [1] + [m * 2 ** (l - 1) // p for l in range(1, L + 1)]
            esum = exps[0].sum(axis=-1)
            for l in range(1, L + 1):
                s_l = exps[l].sum(axis=-1)
                esum = esum + (s_l * scales[l] if scale_attn else s_l)
            esum = esum[..., None]
            Cs = [(scales[l] if l > 0 and scale_attn else 1) * exps[l] / esum for l in range(L + 1)]
            C0 = Cs[0].reshape(bh, nb, m, m)
            Cfull = jnp.zeros((bh, nb, m, 2 * m), C0.dtype).at[:, :, qg, kg].set(C0)
            Vc = v.reshape(bh, nb, m, d)
            Vwin = jnp.concatenate([_shift_prev(Vc), Vc], axis=2)
            out = jnp.einsum('bcqk,bckd->bcqd', Cfull, Vwin).reshape(bh, n, d)
            for l in range(1, L + 1):
                w = m * 2 ** (l - 1)
                nbl = n // w
                Vprev = _shift_prev(Vls[l].reshape(bh, nbl, p, d))
                out = out + jnp.einsum('bcwp,bcpd->bcwd', Cs[l].reshape(bh, nbl, w, p), Vprev).reshape(bh, n, d)
            return out
        B, T, C = x.shape
        H = N_HEAD
        dh = C // H
        qkv = x @ W_attn + b_attn
        q, k, v = jnp.split(qkv, 3, axis=2)

        def heads(t):
            return t.reshape(B, T, H, dh).transpose(0, 2, 1, 3).reshape(B * H, T, dh)
        o = _mla(heads(q), heads(k), heads(v), M_WIN, P, L_LEV, scale_attn=True)
        o = o.reshape(B, H, T, dh).transpose(0, 2, 1, 3).reshape(B, T, C)
        return o @ W_proj + b_proj

    def _L2_ffn_ref(hidden_states, W, b, lora_down, lora_up, down_aux, up_aux):
        import jax, jax.numpy as jnp
        import numpy as np
        ALPHA = 1.0
        lilora_weight = up_aux @ (lora_up @ (lora_down @ down_aux))
        base = jnp.einsum('bsi,oi->bso', hidden_states, W) + b
        delta = jnp.einsum('bsi,oi->bso', hidden_states, lilora_weight)
        return base + ALPHA * delta

    def _L3_attn_ref(x, Wq, Wk, Wv, Wo, fmq_w, fmq_b, fmk_w, fmk_b, rms_w):
        import jax, jax.numpy as jnp
        import numpy as np
        B, N, D = (4, 256, 128)
        H = 8
        DK = D // H
        DV = D // H
        DF = 2 * DK
        CHUNK = 64
        RMS_EPS = 1e-05

        def _hedgehog(x, w, b):
            y = jnp.einsum('bhnd,ed->bhne', x, w) + b
            return jnp.concatenate([jnp.exp(y), jnp.exp(-y)], axis=-1)

        def _fused_chunk_linear_attn(q, k, v):
            b, h, n, df = q.shape
            dv = v.shape[-1]
            nc = n // CHUNK

            def to_chunks(t):
                d = t.shape[-1]
                return t.reshape(b, h, nc, CHUNK, d).transpose(2, 0, 1, 3, 4)
            qc, kc, vc = (to_chunks(q), to_chunks(k), to_chunks(v))
            mask = jnp.tril(jnp.ones((CHUNK, CHUNK), dtype=bool))

            def step(S, inp):
                qi, ki, vi = inp
                attn = jnp.einsum('bhcd,bhed->bhce', qi, ki)
                attn = jnp.where(mask, attn, 0.0)
                intra = jnp.einsum('bhce,bhev->bhcv', attn, vi)
                inter = jnp.einsum('bhcd,bhdv->bhcv', qi, S)
                S = S + jnp.einsum('bhcd,bhcv->bhdv', ki, vi)
                return (S, intra + inter)
            S0 = jnp.zeros((b, h, df, dv), dtype=q.dtype)
            _, oc = jax.lax.scan(step, S0, (qc, kc, vc))
            return oc.transpose(1, 2, 0, 3, 4).reshape(b, h, n, dv)
        b, n, d = x.shape
        split = lambda t: t.reshape(b, n, H, -1).transpose(0, 2, 1, 3)
        q = split(x @ Wq.T)
        k = split(x @ Wk.T)
        v = split(x @ Wv.T)
        q = _hedgehog(q, fmq_w, fmq_b)
        k = _hedgehog(k, fmk_w, fmk_b)
        scale = q.shape[-1] ** (-0.5)
        o = _fused_chunk_linear_attn(q * scale, k, v)
        o = o * jax.lax.rsqrt(jnp.mean(o * o, axis=-1, keepdims=True) + RMS_EPS) * rms_w
        o = o.transpose(0, 2, 1, 3).reshape(b, n, H * DV)
        return o @ Wo.T

    def _L3_ffn_ref(x, Wqkv, q_scale, k_scale, Wo, ln_g, ln_b, W1, b1, W2, b2):
        import jax, jax.numpy as jnp
        import numpy as np
        DIM = 128
        DEPTH = 6
        HEADS = 16
        DIM_HEAD = 64
        WINDOW = 32
        INNER = HEADS * DIM_HEAD
        DIM_INNER = int(DIM * 4 * 2 / 3)
        QK_SCALE = 8.0

        def shift_tokens(t):
            a, s = jnp.split(t, 2, -1)
            s = jnp.pad(s, ((0, 0), (1, 0), (0, 0)))[:, :-1]
            return jnp.concatenate([a, s], -1)

        def l2norm(t):
            return t / jnp.maximum(jnp.linalg.norm(t, axis=-1, keepdims=True), 1e-12)

        def rotate_half(x):
            x1, x2 = jnp.split(x, 2, -1)
            return jnp.concatenate([-x2, x1], -1)

        def rotary_tables(n):
            half = jnp.arange(0, DIM_HEAD, 2, dtype=jnp.float32)
            inv_freq = 1.0 / 10000.0 ** (half / DIM_HEAD)
            t = jnp.arange(n, dtype=jnp.float32)
            freqs = t[:, None] * inv_freq[None, :]
            freqs = jnp.concatenate([freqs, freqs], -1)
            base_scale = (half + 0.4 * DIM_HEAD) / (1.4 * DIM_HEAD)
            power = (t - n // 2) / (WINDOW // 2)
            scale = base_scale[None, :] ** power[:, None]
            scale = jnp.concatenate([scale, scale], -1)
            return (freqs, scale)

        def local_attention(q, k, v):
            b, h, n, d = q.shape
            w = WINDOW
            nw = n // w
            bq = q.reshape(b, h, nw, w, d)
            bk = k.reshape(b, h, nw, w, d)
            bv = v.reshape(b, h, nw, w, d)

            def look(t):
                p = jnp.pad(t, ((0, 0), (0, 0), (1, 0), (0, 0), (0, 0)))
                return jnp.concatenate([p[:, :, :nw], p[:, :, 1:]], axis=3)
            bk2, bv2 = (look(bk), look(bv))
            seq = jnp.arange(n).reshape(nw, w)
            seq_p = jnp.pad(seq, ((1, 0), (0, 0)), constant_values=-1)
            jt = jnp.concatenate([seq_p[:nw], seq_p[1:]], axis=1)
            it = seq[:, :, None]
            jb = jt[:, None, :]
            mask = (it < jb) | (it > jb + w) | (jb == -1)
            sim = jnp.einsum('bhwie,bhwje->bhwij', bq, bk2) * QK_SCALE
            sim = jnp.where(mask, -jnp.finfo(sim.dtype).max, sim)
            attn = jax.nn.softmax(sim, -1)
            out = jnp.einsum('bhwij,bhwje->bhwie', attn, bv2)
            return out.reshape(b, h, n, d)

        def attn_layer(x, Wqkv, qs, ksc, Wo):
            b, n, _ = x.shape
            qkv = x @ Wqkv
            q, k, v = jnp.split(qkv, 3, -1)
            sh = lambda t: t.reshape(b, n, HEADS, DIM_HEAD).transpose(0, 2, 1, 3)
            q, k, v = (sh(q), sh(k), sh(v))
            q = l2norm(q) * qs
            k = l2norm(k) * ksc
            freqs, scale = rotary_tables(n)
            cos, sin = (jnp.cos(freqs), jnp.sin(freqs))
            q = q * cos * scale + rotate_half(q) * sin * scale
            inv = 1.0 / scale
            k = k * cos * inv + rotate_half(k) * sin * inv
            out = local_attention(q, k, v)
            out = out.transpose(0, 2, 1, 3).reshape(b, n, INNER)
            return out @ Wo

        def ffn_layer(x, g, bln, W1, b1, W2, b2):
            mu = x.mean(-1, keepdims=True)
            var = ((x - mu) ** 2).mean(-1, keepdims=True)
            xn = (x - mu) / jnp.sqrt(var + 1e-05) * g + bln
            hg = xn @ W1 + b1
            a, gate = jnp.split(hg, 2, -1)
            return a * jax.nn.gelu(gate, approximate=False) @ W2 + b2
        for i in range(DEPTH):
            x = attn_layer(shift_tokens(x), Wqkv[i], q_scale[i], k_scale[i], Wo[i]) + x
            x = ffn_layer(shift_tokens(x), ln_g[i], ln_b[i], W1[i], b1[i], W2[i], b2[i]) + x
        return x
    x = L0_attn_x
    x = _layernorm(x + _L0_attn_ref(x, L0_attn_Wq, L0_attn_bq, L0_attn_Wk, L0_attn_bk, L0_attn_Wv, L0_attn_bv, L0_attn_Wo, L0_attn_bo, L0_attn_et_gate, L0_attn_is_gate, L0_attn_time_bias), axis=-1)
    x = _layernorm(x + _L0_ffn_ref(x, L0_ffn_w1, L0_ffn_b1, L0_ffn_w2, L0_ffn_b2), axis=-1)
    x = _layernorm(x + _L1_attn_ref(x, L1_attn_Wq, L1_attn_Wk, L1_attn_Wv, L1_attn_Wo), axis=-1)
    x = _layernorm(x + _L1_ffn_ref(x, L1_ffn_gate_w, L1_ffn_w1, L1_ffn_w2), axis=-1)
    x = _layernorm(x + _L2_attn_ref(x, L2_attn_W_attn, L2_attn_b_attn, L2_attn_W_proj, L2_attn_b_proj), axis=-1)
    x = _layernorm(x + _L2_ffn_ref(x, L2_ffn_W, L2_ffn_b, L2_ffn_lora_down, L2_ffn_lora_up, L2_ffn_down_aux, L2_ffn_up_aux), axis=-1)
    x = _layernorm(x + _L3_attn_ref(x, L3_attn_Wq, L3_attn_Wk, L3_attn_Wv, L3_attn_Wo, L3_attn_fmq_w, L3_attn_fmq_b, L3_attn_fmk_w, L3_attn_fmk_b, L3_attn_rms_w), axis=-1)
    x = _layernorm(x + _L3_ffn_ref(x, L3_ffn_Wqkv, L3_ffn_q_scale, L3_ffn_k_scale, L3_ffn_Wo, L3_ffn_ln_g, L3_ffn_ln_b, L3_ffn_W1, L3_ffn_b1, L3_ffn_W2, L3_ffn_b2), axis=-1)
    return x

_drawn_inputs = setup_inputs


def setup_inputs(seed=0):
    import zlib

    import numpy as np

    out = dict(_drawn_inputs(seed))
    spreads = {'L0_attn_bq': (0.0, 0.8),
     'L0_attn_bk': (0.0, 2.0),
     'L0_attn_bv': (0.0, 0.1),
     'L0_attn_bo': (0.0, 0.1),
     'L2_attn_b_attn': (0.0, 0.1),
     'L2_attn_b_proj': (0.0, 0.1),
     'L3_ffn_q_scale': (1.0, 0.6),
     'L3_ffn_k_scale': (1.0, 0.6),
     'L3_ffn_ln_g': (1.0, 0.6),
     'L3_ffn_ln_b': (0.0, 0.8),
     'L3_ffn_b1': (0.0, 0.8),
     'L3_ffn_b2': (0.0, 0.1)}
    factors = {'L0_attn_Wq': 8.0,
     'L0_attn_Wk': 8.0,
     'L0_attn_Wv': 8.0,
     'L0_attn_time_bias': 8.0,
     'L0_ffn_b1': 2.919,
     'L1_attn_Wq': 47.825,
     'L1_attn_Wk': 36.738,
     'L1_ffn_gate_w': 6.414,
     'L1_ffn_w1': 5.734,
     'L1_ffn_w2': 4.879,
     'L2_attn_W_attn': 4.457,
     'L2_ffn_lora_down': 4.25,
     'L2_ffn_lora_up': 4.623,
     'L2_ffn_down_aux': 3.825,
     'L2_ffn_up_aux': 4.096,
     'L3_attn_fmq_b': 8.0,
     'L3_attn_fmk_b': 8.0,
     'L3_ffn_W1': 3.478,
     'L3_ffn_W2': 3.444,
     'L1_attn_Wv': 3.508,
     'L2_ffn_b': 2.704}
    for name, (base, spread) in spreads.items():
        noise = np.random.default_rng([zlib.crc32(name.encode()), seed]).standard_normal(out[name].shape)
        drawn = base * np.exp(spread * noise) if base else spread * noise
        out[name] = jnp.asarray(drawn.astype(out[name].dtype))
    for name, factor in factors.items():
        out[name] = (out[name] * factor).astype(out[name].dtype)
    return out
```

```python
from contextlib import ExitStack

import numpy as np
import concourse.bass as bass
import concourse.mybir as mybir

F32 = mybir.dt.float32
BF16 = mybir.dt.bfloat16
ALU = mybir.AluOpType
ACT = mybir.ActivationFunctionType
AX = mybir.AxisListType

P = 128
D = 128
BATCH, SEQ = 4, 1024
NT = BATCH * SEQ // P
TB = SEQ // P
CH = 512
NCH = BATCH * SEQ // CH
NEG = -1e30


class Shared:
    pass


class Phase:
    used = []

    def __init__(self, nc, name):
        self.nc, self.name, self.stack, self.sems = nc, name, ExitStack(), []

    def __enter__(self):
        return self

    def sb(self, name, shape, dt=F32):
        return self.stack.enter_context(self.nc.sbuf_tensor(f"{self.name}_{name}", shape, dt))

    def ps(self, name, shape, dt=F32):
        return self.stack.enter_context(self.nc.psum_tensor(f"{self.name}_p_{name}", shape, dt))

    def sem(self, name):
        s = self.nc.alloc_semaphore(f"{self.name}_{name}")
        self.sems.append(s)
        return s

    def two(self, name):
        return [self.sem(f"{name}{i}") for i in range(2)]

    def clear_before(self, eng):
        while Phase.used:
            s = Phase.used.pop()
            eng.sem_clear(s)
            self.nc.release_semaphore(s)

    def __exit__(self, *error):
        assert not Phase.used or error[0], "a stage that doesn't clear the semaphores of the one before"
        Phase.used.extend(self.sems)
        self.stack.__exit__(*error)
        return False


def clear_now(nc):
    with Phase(nc, "clear") as ph:
        with nc.Block() as block:
            @block.sync
            def _(sp):
                ph.clear_before(sp)


def across(ap, n):
    return ap.unsqueeze(2).to_broadcast([ap.shape[0], ap.shape[1], n])


def layer_norm(nc, g, transposed=True):
    with Phase(nc, nc.get_next_instruction_name()) as ph:
        centred = ph.sb("centred", [P, 2, TB, D])
        squares = ph.sb("squares", [P, 2, TB, D])
        normed = ph.sb("normed", [P, 2, TB, D])
        total = ph.sb("total", [P, 2, TB])
        mean = ph.sb("mean", [P, 2, TB])
        power = ph.sb("power", [P, 2, TB])
        variance = ph.sb("variance", [P, 2, TB])
        rstd = ph.sb("rstd", [P, 2, TB])
        turned = [ph.ps(f"turned{i}", [P, TB * P]) for i in range(2)]
        s_total, s_mean, s_centred = ph.two("total"), ph.two("mean"), ph.two("centred")
        s_square, s_power, s_var, s_rstd = ph.two("square"), ph.two("power"), ph.two("var"), ph.two("rstd")
        s_normed, s_kept, s_turned, s_xT = ph.two("normed"), ph.two("kept"), ph.two("turned"), ph.two("xT")
        with nc.Block() as block:
            @block.sync
            def _(sp):
                ph.clear_before(sp)

            @block.vector
            def _(dve):
                with dve.Fori(0, BATCH // 2) as it:
                    for s in range(2):
                        y = g.x_tok[:, bass.ds((it * 2 + s) * TB, TB), :]
                        dve.tensor_reduce(total[:, s, :], y, AX.X, ALU.add).then_inc(s_total[s], 1)
                        dve.wait_ge(s_total[s], it + 1)
                        dve.tensor_scalar(mean[:, s, :], total[:, s, :], 1.0 / D, None, ALU.mult).then_inc(s_mean[s], 1)
                        dve.wait_ge(s_mean[s], it + 1)
                        dve.tensor_tensor(centred[:, s], y, across(mean[:, s, :], D), ALU.subtract)\
                           .then_inc(s_centred[s], 1)
                    for s in range(2):
                        dve.wait_ge(s_square[s], it + 1)
                        dve.tensor_reduce(power[:, s, :], squares[:, s], AX.X, ALU.add).then_inc(s_power[s], 1)
                        dve.wait_ge(s_power[s], it + 1)
                        dve.tensor_scalar(variance[:, s, :], power[:, s, :], 1.0 / D, 1e-5, ALU.mult, ALU.add)\
                           .then_inc(s_var[s], 1)
                    for s in range(2):
                        dve.wait_ge(s_rstd[s], it + 1)
                        dve.wait_ge(s_kept[s], it)
                        if transposed:
                            dve.wait_ge(s_turned[s], it)
                        dve.tensor_tensor(normed[:, s], centred[:, s], across(rstd[:, s, :], D), ALU.mult)\
                           .then_inc(s_normed[s], 1)

            @block.gpsimd
            def _(pool):
                with pool.Fori(0, BATCH // 2) as it:
                    for s in range(2):
                        pool.wait_ge(s_var[s], it + 1)
                        pool.tensor_tensor(rstd[:, s, :], variance[:, s, :], g.minus_half[:, 0:TB], ALU.pow)\
                            .then_inc(s_rstd[s], 1)

            @block.scalar
            def _(act):
                with act.Fori(0, BATCH // 2) as it:
                    for s in range(2):
                        act.wait_ge(s_centred[s], it + 1)
                        act.activation(squares[:, s], centred[:, s], ACT.Square).then_inc(s_square[s], 1)
                    for s in range(2):
                        act.wait_ge(s_normed[s], it + 1)
                        act.activation(g.x_tok[:, bass.ds((it * 2 + s) * TB, TB), :], normed[:, s], ACT.Copy)\
                           .then_inc(s_kept[s], 1)
                        if transposed:
                            act.wait_ge(s_turned[s], it + 1)
                            act.activation(g.xT[:, bass.ds((it * 2 + s) * SEQ, SEQ)], turned[s][:], ACT.Copy)\
                               .then_inc(s_xT[s], 1)

            if transposed:
                @block.tensor
                def _(pe):
                    with pe.Fori(0, BATCH // 2) as it:
                        for s in range(2):
                            pe.wait_ge(s_normed[s], it + 1)
                            pe.wait_ge(s_xT[s], it)
                            for j in range(TB):
                                mm = pe.transpose(turned[s][:, j * P:(j + 1) * P], normed[:, s, j, :], g.ident[:])
                            mm.then_inc(s_turned[s], 1)


def load_constants(nc, g):
    with Phase(nc, "start") as ph:
        s_in, s_half = ph.sem("in"), ph.sem("half")
        with nc.Block() as block:
            @block.sync
            def _(sp):
                sp.dma_start(g.x_tok[:], g.dram["L0_attn_x"].rearrange("n (j p) d -> p (n j) d", p=P)).then_inc(s_in, 16)
                sp.dma_start(g.ident[:], g.dram["c_ident"][:, :]).then_inc(s_in, 16)
                sp.wait_ge(s_in, 32)
                ph.clear_before(sp)

            @block.gpsimd
            def _(pool):
                pool.memset(g.minus_half[:], -0.5).then_inc(s_half, 1)
                pool.memset(g.ones[:], 1.0).then_inc(s_half, 1)


def store_output(nc, g):
    with Phase(nc, "end") as ph:
        s_out = ph.sem("out")
        with nc.Block() as block:
            @block.sync
            def _(sp):
                sp.dma_start(g.dram["out"].rearrange("n (j p) d -> p (n j) d", p=P), g.x_tok[:]).then_inc(s_out, 16)
                sp.wait_ge(s_out, 16)
                ph.clear_before(sp)


BIAS_HEADS, BIAS_DH = 16, 8
TERMS = 9
VW = BIAS_DH + 1
REACH = SEQ + TB - 1
MIXED_TILES = 4
BIAS_SCALE = BIAS_DH ** -0.5


def project(nc, g):
    with Phase(nc, "prj") as ph:
        w = ph.sb("w", [P, 3, D])
        bias = ph.sb("bias", [P, 2])
        bias_q = ph.sb("bias_q", [P, 1])
        bv = ph.sb("bv", [1, D])
        gates = ph.sb("gates", [P, 2])
        grown = ph.sb("grown", [P, 1])
        plus1 = ph.sb("plus1", [P, 1])
        factor = ph.sb("factor", [P, 1])
        shift = ph.sb("shift", [P, 1])
        raw_bias = ph.sb("raw_bias", [P, REACH])
        xs = ph.sb("xs", [P, 2, CH])
        whole = ph.sb("whole", [P, 2, CH])
        rest = ph.sb("rest", [P, 2, CH])
        parts = ph.sb("parts", [P, 2, 2, 3, CH], BF16)
        p_q = [ph.ps(f"q{i}", [P, CH]) for i in range(2)]
        p_v = ph.ps("v", [P, CH])
        s_in, s_xT, s_xs, s_m, s_w, s_r, s_v, s_vc, s_st = (
            ph.sem(n) for n in ("in", "xT", "xs", "m", "w", "r", "v", "vc", "st"))
        s_p1, s_p2, s_p3 = ph.sem("p1"), ph.sem("p2"), ph.sem("p3")
        s_e, s_one, s_f, s_n, s_tab, s_bq = (ph.sem(n) for n in ("e", "one", "f", "n", "tab", "bq"))
        INS = 6
        STORES = 8
        with nc.Block() as block:
            @block.sync
            def _(sp):
                sp.dma_start(g.xT[:], g.dram["L0_attn_xT"][:, :]).then_inc(s_xT, 16)
                sp.dma_start(w[:], g.dram["L0_attn_wT"][:, :, :]).then_inc(s_in, 16)
                sp.dma_start(bias[:], g.dram["L0_attn_bqk"][:, :]).then_inc(s_in, 16)
                sp.dma_start(bv[:], g.dram["L0_attn_bv_row"][:, :]).then_inc(s_in, 16)
                sp.dma_start(raw_bias[:], g.dram["L0_attn_bias"][:, :]).then_inc(s_in, 16)
                for i, of in enumerate((g.dram["L0_attn_et_gate"], g.dram["L0_attn_is_gate"])):
                    sp.dma_start(gates[:, i:i + 1], of.rearrange("a b c -> (a b c)").partition_broadcast(P))\
                      .then_inc(s_in, 16)
                with sp.Fori(0, BATCH) as b:
                    for u in range(2):
                        c = b * 2 + u
                        sp.wait_ge(s_st, c * (16 * STORES))
                        sp.wait_ge(s_p3, c * 2 + 2)
                        rows, cols = bass.ds(b * P, P), slice(u * CH, (u + 1) * CH)
                        for n in range(3):
                            sp.dma_start(g.q_terms[rows, 3 * n:3 * n + 3, cols], parts[:, u, 0]).then_inc(s_st, 16)
                            sp.dma_start(g.k_terms[rows, 3 * n:3 * n + 3 - n, cols], parts[:, u, 1, n:3]).then_inc(s_st, 16)
                            if n:
                                sp.dma_start(g.k_terms[rows, 3 * n + 3 - n:3 * n + 3, cols], parts[:, u, 1, 0:n])\
                                  .then_inc(s_st, 16)

                sp.wait_ge(s_st, NCH * 16 * STORES)
                ph.clear_before(sp)

            @block.tensor
            def _(pe):
                with pe.Fori(0, BATCH) as b:
                    for u in range(2):
                        c = b * 2 + u
                        pe.wait_ge(s_xs, c + 1)
                        for n in range(2):
                            pe.wait_ge(s_w, c * 2)
                            pe.matmul(p_q[n][:], w[:, n, :], xs[:, u, :], start=True, stop=True).then_inc(s_m, 1)
                        pe.wait_ge(s_vc, c)
                        for j in range(CH // P):
                            at = p_v[:, j * P:(j + 1) * P]
                            pe.matmul(at, xs[:, u, j * P:(j + 1) * P], w[:, 2, :], start=True, stop=False)
                            mm = pe.matmul(at, g.ones[0:1, :], bv[:], start=False, stop=True)
                        mm.then_inc(s_v, 1)

            @block.gpsimd
            def _(pool):
                pool.wait_ge(s_xT, 16)
                pool.wait_ge(s_in, 16 * INS)
                with pool.Fori(0, BATCH) as b:
                    for u in range(2):
                        c = b * 2 + u
                        pool.wait_ge(s_v, b)
                        pool.wait_ge(s_vc, c)
                        pool.tensor_copy(xs[:, u, :], g.xT[:, bass.ds(c * CH, CH)]).then_inc(s_xs, 1)

            @block.scalar
            def _(act):
                act.wait_ge(s_in, 16 * INS)
                act.activation(grown[:], gates[:, 0:1], ACT.Exp, scale=-1.0).then_inc(s_e, 1)
                act.activation(bias_q[:], bias[:, 0:1], ACT.Copy, scale=-BIAS_SCALE).then_inc(s_bq, 1)
                act.wait_ge(s_bq, 1)
                with act.Fori(0, BATCH) as b:
                    for u in range(2):
                        c = b * 2 + u
                        for n in range(2):
                            act.wait_ge(s_m, c * 2 + (n + 1))
                            act.wait_ge(s_r, c * 2)
                            act.wait_ge(s_p1, c * 2)
                            act.activation(whole[:, n, :], p_q[n][:], ACT.Identity, bias=(bias_q[:], bias[:, 1:2])[n],
                                           scale=(-BIAS_SCALE, 1.0)[n]).then_inc(s_w, 1)
                        for n in range(2):
                            act.wait_ge(s_w, c * 2 + (n + 1))
                            act.wait_ge(s_st, b * (2 * 16 * STORES))
                            act.activation(parts[:, u, n, 0, :], whole[:, n, :], ACT.Copy).then_inc(s_p1, 1)
                        act.wait_ge(s_v, c + 1)
                        act.activation(g.v_all[:, :, bass.ds(b, 1), u * MIXED_TILES:(u + 1) * MIXED_TILES, :]
                                       .rearrange("p h a j d -> p (a j) h d"),
                                       p_v[:].rearrange("p (j h d) -> p j h d", h=BIAS_HEADS, d=BIAS_DH), ACT.Copy).then_inc(s_vc, 1)

            @block.vector
            def _(dve):
                dve.wait_ge(s_e, 1)
                dve.tensor_scalar(plus1[:], grown[:], 1.0, None, ALU.add).then_inc(s_one, 1)
                dve.wait_ge(s_one, 1)
                dve.reciprocal(factor[:], plus1[:]).then_inc(s_f, 1)
                dve.tensor_scalar(shift[:], gates[:, 1:2], -1.0, None, ALU.mult).then_inc(s_n, 1)
                dve.wait_ge(s_f, 1)
                dve.tensor_scalar(raw_bias[:], raw_bias[:], factor[:], -1.0, ALU.mult, ALU.mult).then_inc(s_tab, 1)
                dve.wait_ge(s_tab, 1)
                dve.wait_ge(s_n, 1)
                dve.tensor_scalar(g.time_bias[:], raw_bias[:], shift[:], None, ALU.add)
                with dve.Fori(0, BATCH) as b:
                    for u in range(2):
                        c = b * 2 + u
                        for n in range(2):
                            dve.wait_ge(s_p1, c * 2 + (n + 1))
                            dve.wait_ge(s_p3, c * 2)
                            dve.tensor_tensor(rest[:, n, :], whole[:, n, :], parts[:, u, n, 0, :], ALU.subtract)\
                               .then_inc(s_r, 1)
                        for n in range(2):
                            dve.wait_ge(s_r, c * 2 + (n + 1))
                            dve.tensor_copy(parts[:, u, n, 1, :], rest[:, n, :]).then_inc(s_p2, 1)
                        for n in range(2):
                            dve.wait_ge(s_p2, c * 2 + (n + 1))
                            dve.tensor_tensor(parts[:, u, n, 2, :], rest[:, n, :], parts[:, u, n, 1, :], ALU.subtract)\
                               .then_inc(s_p3, 1)


def attend(nc, g):
    PAIRS = BATCH * BIAS_HEADS
    KT = SEQ // P
    GROUPS = TB // MIXED_TILES
    HALF = KT // 2
    with Phase(nc, "att") as ph:
        q = ph.sb("q", [TERMS * BIAS_DH, 2, SEQ], BF16)
        k = ph.sb("k", [TERMS * BIAS_DH, 2, SEQ], BF16)
        v = ph.sb("v", [P, KT, VW])
        biased = ph.sb("biased", [P, 2, SEQ])
        least = ph.sb("least", [P, 2])
        probs = ph.sb("probs", [P, 2, SEQ])
        pT = ph.sb("pT", [P, 2, KT, MIXED_TILES * P])
        o = ph.sb("o", [VW, 2, CH])
        share = ph.sb("share", [P, 2, MIXED_TILES])
        out = ph.sb("out", [P, 2, MIXED_TILES, BIAS_DH])
        p_s = [ph.ps(f"s{i}", [P, SEQ]) for i in range(2)]
        p_t = [ph.ps(f"t{i}", [P, CH]) for i in range(2)]
        p_o = ph.ps("o", [VW, CH])
        p_b = ph.ps("b", [P, 2, MIXED_TILES, VW])
        s_b, s_share, s_out = ph.sem("b"), ph.sem("share"), ph.sem("out")
        s_qk, s_v, s_one, s_s, s_x, s_e = (ph.sem(n) for n in ("qk", "v", "one", "s", "x", "e"))
        s_t, s_c = ph.two("t"), ph.two("c")
        s_o, s_oc, s_st = ph.sem("o"), ph.sem("oc"), ph.sem("st")

        def pairs(eng, prologue, body):
            prologue()
            body(0, False, True)
            with eng.Fori(0, PAIRS - 2) as i:
                body(i + 1, True, True)
            body(PAIRS - 1, True, False)

        with nc.Block() as block:
            @block.sync
            def _(sp):
                def load(pair, slot):
                    head, sequence = pair >> 2, pair & 3
                    for to, of in ((q, g.q_terms), (k, g.k_terms)):
                        sp.dma_start(to[:, slot, :], of[bass.ds(sequence * P + head * BIAS_DH, BIAS_DH), :, :].rearrange("d t n -> (d t) n"))\
                          .then_inc(s_qk, 16)

                def store(pair):
                    sp.dma_start(g.mixed[bass.ds(pair, 1), :, :].rearrange("a (p t) d -> p (a t d)", t=TB),
                                 out[:].rearrange("p n t d -> p (n t d)")).then_inc(s_st, 16)

                def body(before, slot):
                    sp.wait_ge(s_st, before * 16)
                    sp.wait_ge(s_qk, before * 32 + 96)
                    sp.wait_ge(s_s, before * TB + 2 * TB)
                    sp.wait_ge(s_out, before * GROUPS + GROUPS)
                    store(before)
                    load(before + 3, slot)

                load(0, 0)
                sp.wait_ge(s_qk, 32)
                load(1, 1)
                sp.wait_ge(s_qk, 64)
                sp.wait_ge(s_s, TB)
                load(2, 0)
                with sp.Fori(0, PAIRS // 2 - 2) as it:
                    for u in range(2):
                        body(it * 2 + u, 1 - u)
                body(PAIRS - 4, 1)
                for pair in range(PAIRS - 3, PAIRS):
                    sp.wait_ge(s_st, pair * 16)
                    sp.wait_ge(s_out, pair * GROUPS + GROUPS)
                    store(pair)
                sp.wait_ge(s_st, PAIRS * 16)
                ph.clear_before(sp)

            @block.tensor
            def _(pe):
                def scores(pair, t):
                    if t == 0:
                        pe.wait_ge(s_qk, pair * 32 + 32)
                    pe.wait_ge(s_x, pair * TB + (t - 1) if not (isinstance(pair, int) and pair == 0 and t < 2) else 0)
                    slot = pair & 1
                    at = (lambda m, n, w: m[:, slot, n:n + w]) if isinstance(pair, int) else \
                         (lambda m, n, w: m[:, bass.ds(slot, 1), n:n + w].rearrange("r a n -> r (a n)"))
                    queries = at(q, 0, SEQ).rearrange("r (p t) -> r t p", t=TB)[:, t, :]
                    for n in range(2):
                        mm = pe.matmul(p_s[t % 2][:, n * CH:(n + 1) * CH], queries, at(k, n * CH, CH), start=True, stop=True)
                    mm.then_inc(s_s, 1)

                def turn(pair, t):
                    pe.wait_ge(s_e, pair * TB + (t + 1))
                    for n in range(2):
                        pe.wait_ge(s_c[n], pair * TB + t)
                        for j in range(HALF):
                            kt = n * HALF + j
                            mm = pe.transpose(p_t[n][:, j * P:(j + 1) * P], probs[:, t % 2, kt * P:(kt + 1) * P], g.ident[:])
                        mm.then_inc(s_t[n], 1)

                def mix(pair, n, part):
                    if part == 0:
                        pe.wait_ge(s_v, pair + 1)
                        pe.wait_ge(s_oc, pair * GROUPS + n)
                    for kt in (2 * part, 2 * part + 1):
                        if kt % HALF == 0:
                            pe.wait_ge(s_c[kt // HALF], pair * TB + (n + 1) * MIXED_TILES)
                        mm = pe.matmul(p_o[:], v[:, kt, :], pT[:, n, kt, :], start=(kt == 0), stop=(kt == KT - 1))
                    if part == KT // 2 - 1:
                        mm.then_inc(s_o, 1)

                def turn_back(pair, n):
                    pe.wait_ge(s_oc, pair * GROUPS + (n + 1))
                    pe.wait_ge(s_out, pair * GROUPS + n)
                    for j in range(MIXED_TILES):
                        mm = pe.matmul(p_b[:, n, j, :], o[:, n, j * P:(j + 1) * P], g.ident[0:VW, 0:VW], start=True, stop=True)
                    mm.then_inc(s_b, 1)

                def body(pair, before, more):
                    for t in range(TB):
                        turn(pair, t)
                        if t + 2 < TB:
                            scores(pair, t + 2)
                        elif more:
                            scores(pair + 1, t + 2 - TB)
                        if t >= MIXED_TILES:
                            mix(pair, 0, t - MIXED_TILES)
                        elif before:
                            mix(pair - 1, 1, t)
                        if before and t % MIXED_TILES == 1:
                            turn_back(pair - 1, t // MIXED_TILES)
                    if not more:
                        turn_back(pair, 0)
                        for part in range(KT // 2):
                            mix(pair, 1, part)
                        turn_back(pair, 1)

                def prologue():
                    scores(0, 0)
                    scores(0, 1)

                pairs(pe, prologue, body)

            @block.vector
            def _(dve):
                def wait_scores(pair, t):
                    dve.wait_ge(s_s, pair * TB + (t + 1))
                    if not (isinstance(pair, int) and pair == 0 and t < 2):
                        dve.wait_ge(s_e, pair * TB + (t - 1))

                def add_bias(t):
                    dve.tensor_tensor_reduce(biased[:, t % 2, :], p_s[t % 2][:], g.time_bias[:, TB - 1 - t:TB - 1 - t + SEQ],
                                             1.0, -NEG, ALU.add, ALU.min, least[:, t % 2:t % 2 + 1]).then_inc(s_x, 1)

                def keep(pair, t):
                    dve.wait_ge(s_t[1], pair * TB + (t + 1))
                    if t >= MIXED_TILES or not (isinstance(pair, int) and pair == 0):
                        dve.wait_ge(s_o, pair * GROUPS + (t // MIXED_TILES - 1))
                    dve.tensor_copy(pT[:, t // MIXED_TILES, HALF:KT, t % MIXED_TILES * P:(t % MIXED_TILES + 1) * P],
                                    p_t[1][:].rearrange("p (k q) -> p k q", q=P)).then_inc(s_c[1], 1)

                def divide(pair, n):
                    dve.wait_ge(s_b, pair * GROUPS + (n + 1))
                    dve.reciprocal(share[:, n, :], p_b[:, n, :, BIAS_DH]).then_inc(s_share, 1)
                    dve.wait_ge(s_share, pair * GROUPS + (n + 1))
                    dve.wait_ge(s_st, pair * 16)
                    dve.tensor_tensor(out[:, n], p_b[:, n, :, 0:BIAS_DH], across(share[:, n, :], BIAS_DH), ALU.mult).then_inc(s_out, 1)

                def body(pair, before, more):
                    for t in range(TB):
                        follows = more or t + 2 < TB
                        if follows:
                            if t + 2 < TB:
                                wait_scores(pair, t + 2)
                            else:
                                wait_scores(pair + 1, t + 2 - TB)
                        keep(pair, t)
                        if follows:
                            add_bias((t + 2) % TB)
                        if before and t % MIXED_TILES == 2:
                            divide(pair - 1, t // MIXED_TILES)
                    if not more:
                        divide(pair, 0)
                        divide(pair, 1)

                def prologue():
                    for t in range(2):
                        wait_scores(0, t)
                        add_bias(t)

                pairs(dve, prologue, body)

            @block.scalar
            def _(act):
                def exponential(pair, t):
                    act.wait_ge(s_x, pair * TB + (t + 1))
                    if not (isinstance(pair, int) and pair == 0 and t < 2):
                        act.wait_ge(s_t[1], pair * TB + (t - 1))
                    act.activation(probs[:, t % 2, :], biased[:, t % 2, :], ACT.Exp, bias=least[:, t % 2:t % 2 + 1], scale=-1.0)\
                       .then_inc(s_e, 1)

                def keep_mixed(pair, n):
                    act.wait_ge(s_o, pair * GROUPS + (n + 1))
                    act.wait_ge(s_b, pair * GROUPS)
                    act.activation(o[:, n, :], p_o[:], ACT.Copy).then_inc(s_oc, 1)

                def body(pair, before, more):
                    for t in range(TB):
                        if t + 1 < TB:
                            exponential(pair, t + 1)
                        elif more:
                            exponential(pair + 1, 0)
                        if before and t % MIXED_TILES == 0:
                            keep_mixed(pair - 1, t // MIXED_TILES)
                        act.wait_ge(s_t[0], pair * TB + (t + 1))
                        if t >= MIXED_TILES or before:
                            act.wait_ge(s_o, pair * GROUPS + (t // MIXED_TILES - 1))
                        act.activation(pT[:, t // MIXED_TILES, 0:HALF, t % MIXED_TILES * P:(t % MIXED_TILES + 1) * P],
                                       p_t[0][:].rearrange("p (k q) -> p k q", q=P), ACT.Copy).then_inc(s_c[0], 1)
                    if not more:
                        keep_mixed(pair, 0)
                        keep_mixed(pair, 1)

                pairs(act, lambda: exponential(0, 0), body)

            @block.gpsimd
            def _(pool):
                pool.memset(v[:], 1.0).then_inc(s_one, 1)
                pool.wait_ge(s_one, 1)

                def values(pair):
                    pool.tensor_copy(v[:, :, 0:BIAS_DH], g.v_all[:].rearrange("p h b j d -> p (h b) j d")[:, bass.ds(pair, 1)].rearrange("p a j d -> p (a j) d")).then_inc(s_v, 1)

                def body(pair, before, more):
                    if more:
                        pool.wait_ge(s_o, pair * GROUPS + GROUPS)
                        values(pair + 1)

                pairs(pool, lambda: values(0), body)


def project_out(nc, g):
    with Phase(nc, "out") as ph:
        woT = ph.sb("woT", [P, D])
        bo = ph.sb("bo", [1, D])
        slot = ph.sb("slot", [P, 2, MIXED_TILES, D])
        mixT = ph.sb("mixT", [P, 2, CH])
        p_t = [ph.ps(f"t{i}", [P, CH]) for i in range(2)]
        p_y = [ph.ps(f"y{i}", [P, CH]) for i in range(2)]
        s_in, s_slot, s_t, s_tc, s_y, s_res = (ph.sem("in"), ph.two("slot"), *(ph.sem(n) for n in ("t", "tc", "y", "res")))
        INS = 2
        with nc.Block() as block:
            @block.sync
            def _(sp):
                sp.dma_start(woT[:], g.dram["L0_attn_woT"][:, :]).then_inc(s_in, 16)
                sp.dma_start(bo[:], g.dram["L0_attn_bo_row"][:, :]).then_inc(s_in, 16)
                rows = g.mixed.rearrange("a (r t) d -> (a r) (t d)", t=D // BIAS_DH)
                with sp.Fori(0, BATCH) as b:
                    for u in range(2):
                        c = b * 2 + u
                        sp.wait_ge(s_t, b * 2)
                        sp.dma_start(slot[:, u], rows[bass.ds(c * CH, CH), :].rearrange("(j p) n -> p j n", p=P))\
                          .then_inc(s_slot[u], 16)
                ph.clear_before(sp)

            @block.tensor
            def _(pe):
                pe.wait_ge(s_in, 16 * INS)
                with pe.Fori(0, BATCH) as b:
                    for u in range(2):
                        c = b * 2 + u
                        pe.wait_ge(s_slot[u], b * 16 + 16)
                        pe.wait_ge(s_tc, b * 2)
                        for j in range(MIXED_TILES):
                            mm = pe.transpose(p_t[u][:, j * P:(j + 1) * P], slot[:, u, j, :], g.ident[:])
                        mm.then_inc(s_t, 1)
                    for u in range(2):
                        c = b * 2 + u
                        pe.wait_ge(s_tc, c + 1)
                        pe.wait_ge(s_res, b * 2)
                        for j in range(MIXED_TILES):
                            at = p_y[u][:, j * P:(j + 1) * P]
                            pe.matmul(at, mixT[:, u, j * P:(j + 1) * P], woT[:], start=True, stop=False)
                            mm = pe.matmul(at, g.ones[0:1, :], bo[:], start=False, stop=True)
                        mm.then_inc(s_y, 1)

            @block.scalar
            def _(act):
                with act.Fori(0, BATCH) as b:
                    for u in range(2):
                        act.wait_ge(s_t, b * 2 + (u + 1))
                        act.wait_ge(s_y, b * 2)
                        act.activation(mixT[:, u, :], p_t[u][:], ACT.Copy).then_inc(s_tc, 1)

            @block.vector
            def _(dve):
                with dve.Fori(0, BATCH) as b:
                    for u in range(2):
                        c = b * 2 + u
                        dve.wait_ge(s_y, c + 1)
                        x = g.x_tok[:, bass.ds(c * MIXED_TILES, MIXED_TILES), :]
                        dve.tensor_tensor(x, p_y[u][:].rearrange("p (j d) -> p j d", d=D), x, ALU.add).then_inc(s_res, 1)


def biased_attention(nc, g):
    def dram(name, shape, dt):
        return nc.dram_tensor(name, shape, dt, kind="Internal").ap()

    g.q_terms = dram("q_terms", (BATCH * P + BIAS_DH, TERMS, SEQ), BF16)
    g.k_terms = dram("k_terms", (BATCH * P + BIAS_DH, TERMS, SEQ), BF16)
    g.mixed = dram("mixed", (BIAS_HEADS * BATCH, SEQ, BIAS_DH), F32)
    with ExitStack() as ctx:
        g.v_all = ctx.enter_context(nc.sbuf_tensor("v_all", [P, BIAS_HEADS, BATCH, TB, BIAS_DH], F32))
        g.time_bias = ctx.enter_context(nc.sbuf_tensor("time_bias", [P, REACH], F32))
        project(nc, g)
        attend(nc, g)
    project_out(nc, g)


def binary_ffn(nc, g):
    HID = 512
    HT = HID // P
    with Phase(nc, "bin") as ph:
        w = ph.sb("w", [P, 2, HID])
        magnitude = ph.sb("magnitude", [P, 2, HID])
        sign = ph.sb("sign", [P, 2, HID])
        alpha = ph.sb("alpha", [P, HT + 1])
        w1T = ph.sb("w1T", [P, HID])
        w2T = ph.sb("w2T", [P, HT, D])
        b1 = ph.sb("b1", [P, HT])
        b2 = ph.sb("b2", [1, D])
        hidden = ph.sb("hidden", [P, 2, HT, CH])
        hid = [ph.ps(f"hid{j}", [P, CH]) for j in range(HT)]
        out = [ph.ps(f"out{i}", [P, CH]) for i in range(2)]
        s_w, s_mag, s_sgn, s_alpha, s_mul = ph.sem("w"), ph.sem("mag"), ph.sem("sgn"), ph.sem("alpha"), ph.sem("mul")
        s_bin, s_turn, s_wT = ph.sem("bin"), ph.sem("turn"), ph.sem("wT")
        s_hid, s_gelu = ph.sem("hid"), ph.sem("gelu")
        s_out, s_sum = ph.two("out"), ph.two("sum")
        with nc.Block() as block:
            @block.sync
            def _(sp):
                sp.dma_start(w[:, 0, :].rearrange("p (j d) -> p j d", j=HT),
                             g.dram["L0_ffn_w1"].rearrange("(j p) d -> p j d", p=P)).then_inc(s_w, 16)
                sp.dma_start(w[:, 1, :], g.dram["L0_ffn_w2"][:, :]).then_inc(s_w, 16)
                sp.dma_start(b1[:], g.dram["L0_ffn_b1T"][:, :]).then_inc(s_w, 16)
                sp.dma_start(b2[:], g.dram["L0_ffn_b2"].rearrange("(a d) -> a d", a=1)).then_inc(s_w, 16)
                ph.clear_before(sp)

            @block.scalar
            def _(act):
                act.wait_ge(s_w, 64)
                act.activation(magnitude[:], w[:], ACT.Abs).then_inc(s_mag, 1)
                act.activation(sign[:], w[:], ACT.Sign).then_inc(s_sgn, 1)

                def gelu(c, s, it):
                    for j in range(HT):
                        act.wait_ge(s_hid, c * HT + (j + 1))
                        act.wait_ge(s_out[s], it)
                        act.activation(hidden[:, s, j, :], hid[j][:], ACT.Gelu, bias=b1[:, j:j + 1])\
                           .then_inc(s_gelu, 1)

                with act.Fori(0, NCH // 2) as it:
                    for s in range(2):
                        gelu(it * 2 + s, s, it)

            @block.vector
            def _(dve):
                dve.wait_ge(s_mag, 1)
                dve.tensor_reduce(alpha[:, 0:HT], magnitude[:, 0, :].rearrange("p (j d) -> p j d", j=HT), AX.X, ALU.add)\
                   .then_inc(s_alpha, 1)
                dve.tensor_reduce(alpha[:, HT:HT + 1], magnitude[:, 1, :], AX.X, ALU.add).then_inc(s_alpha, 1)
                dve.wait_ge(s_alpha, 2)
                dve.wait_ge(s_sgn, 1)
                for j in range(HT):
                    dve.tensor_scalar(magnitude[:, 0, j * D:(j + 1) * D], sign[:, 0, j * D:(j + 1) * D],
                                      alpha[:, j:j + 1], 1.0 / D, ALU.mult, ALU.mult).then_inc(s_mul, 1)
                dve.tensor_scalar(magnitude[:, 1, :], sign[:, 1, :], alpha[:, HT:HT + 1], 1.0 / HID,
                                  ALU.mult, ALU.mult).then_inc(s_mul, 1)
                dve.wait_ge(s_mul, HT + 1)
                dve.tensor_tensor(magnitude[:], magnitude[:], w[:], ALU.subtract).then_inc(s_bin, 1)
                dve.wait_ge(s_bin, 1)
                dve.tensor_tensor(w[:], w[:], magnitude[:], ALU.add).then_inc(s_bin, 1)
                dve.wait_ge(s_turn, 1)
                dve.tensor_copy(w1T[:], hid[0][:]).then_inc(s_wT, 1)
                dve.tensor_copy(w2T[:].rearrange("p j d -> p (j d)"), hid[1][:]).then_inc(s_wT, 1)
                with dve.Fori(0, NCH // 2) as it:
                    for s in range(2):
                        dve.wait_ge(s_out[s], it + 1)
                        x = g.x_tok[:, bass.ds((it * 2 + s) * 4, 4), :]
                        dve.tensor_tensor(x, out[s][:].rearrange("p (i d) -> p i d", i=4), x, ALU.add)\
                           .then_inc(s_sum[s], 1)

            @block.tensor
            def _(pe):
                pe.wait_ge(s_bin, 2)
                for n in range(2):
                    for j in range(HT):
                        mm = pe.transpose(hid[n][:, j * P:(j + 1) * P], w[:, n, j * P:(j + 1) * P], g.ident[:])
                mm.then_inc(s_turn, 1)
                pe.wait_ge(s_wT, 2)

                def up(c, first=False):
                    for j in range(HT):
                        if not first:
                            pe.wait_ge(s_gelu, c * HT + (j + 1 - HT))
                        pe.matmul(hid[j][:], w1T[:, j * P:(j + 1) * P], g.xT[:, bass.ds(c * CH, CH)],
                                  start=True, stop=True).then_inc(s_hid, 1)

                def down(c, s, it):
                    pe.wait_ge(s_gelu, c * HT + HT)
                    pe.wait_ge(s_sum[s], it)
                    for i in range(4):
                        y = out[s][:, i * D:(i + 1) * D]
                        pe.matmul(y, g.ones[0:1, :], b2[:], start=True, stop=False)
                        for j in range(HT):
                            mm = pe.matmul(y, hidden[:, s, j, i * P:(i + 1) * P], w2T[:, j, :],
                                           start=False, stop=(j == HT - 1))
                    mm.then_inc(s_out[s], 1)

                up(0, first=True)
                with pe.Fori(0, NCH // 2 - 1) as it:
                    for s in range(2):
                        up(it * 2 + (s + 1))
                        down(it * 2 + s, s, it)
                up(NCH - 1)
                down(NCH - 2, 0, NCH // 2 - 1)
                down(NCH - 1, 1, NCH // 2 - 1)


def linear_attention(nc, g):
    with Phase(nc, "lin") as ph:
        wkv = ph.sb("wkv", [P, 2 * D])
        wq = ph.sb("wq", [P, D])
        wo = ph.sb("wo", [P, D])
        same_head = ph.sb("same_head", [P, P])
        xs = ph.sb("xs", [P, 2, 2 * P])
        low = ph.sb("low", [P, 2, 2, D])
        expd = ph.sb("expd", [P, 2, 2, D])
        kf = ph.sb("kf", [P, 2, 2, D])
        v = ph.sb("v", [P, 2, 2, D + 1])
        kv = ph.sb("kv", [P, D])
        k1 = ph.sb("k1", [P, D])
        qlow = ph.sb("qlow", [P, CH])
        qexp = ph.sb("qexp", [P, CH])
        qf = ph.sb("qf", [P, CH])
        den = ph.sb("den", [P, CH])
        mixed = ph.sb("mixed", [P, CH])
        p_kv = [ph.ps(f"kv{i}", [P, 2, 2 * D]) for i in range(2)]
        p_sum = ph.ps("sum", [P, D + 1])
        p_q, p_num, p_den, p_y = (ph.ps(n, [P, CH]) for n in ("q", "num", "den", "y"))
        s_in, s_ones = ph.sem("in"), ph.sem("ones")
        s_xs, s_kvp, s_low, s_exp = ph.two("xs"), ph.two("kvp"), ph.two("low"), ph.two("exp")
        s_kf, s_v, s_used = ph.two("kf"), ph.two("v"), ph.two("used")
        s_tot, s_kv = ph.sem("tot"), ph.sem("kv")
        s_q, s_qlow, s_qexp, s_qf = ph.sem("q"), ph.sem("qlow"), ph.sem("qexp"), ph.sem("qf")
        s_nd, s_eps, s_rec, s_mix, s_y, s_res = (ph.sem(n) for n in ("nd", "eps", "rec", "mix", "y", "res"))
        PAIRS = TB // 2
        with nc.Block() as block:
            @block.sync
            def _(sp):
                sp.dma_start(wkv[:, 0:D], g.dram["L1_attn_Wk"][:, :]).then_inc(s_in, 16)
                sp.dma_start(wkv[:, D:2 * D], g.dram["L1_attn_Wv"][:, :]).then_inc(s_in, 16)
                sp.dma_start(wq[:], g.dram["L1_attn_Wq"][:, :]).then_inc(s_in, 16)
                sp.dma_start(wo[:], g.dram["L1_attn_Wo"][:, :]).then_inc(s_in, 16)
                sp.dma_start(same_head[:], g.dram["c_same_head8"][:, :]).then_inc(s_in, 16)
                ph.clear_before(sp)

            @block.gpsimd
            def _(pool):
                pool.memset(v[:], 1.0).then_inc(s_ones, 1)
                with pool.Fori(0, BATCH) as b:
                    for t in range(PAIRS):
                        s, n = t % 2, t // 2
                        pool.wait_ge(s_kvp[s], b * 2 + n)
                        pool.tensor_copy(xs[:, s, :], g.xT[:, bass.ds(b * SEQ + t * 2 * P, 2 * P)]).then_inc(s_xs[s], 1)

            @block.tensor
            def _(pe):
                pe.wait_ge(s_in, 80)
                with pe.Fori(0, BATCH) as b:
                    def project(t):
                        s, n = t % 2, t // 2
                        pe.wait_ge(s_xs[s], b * 2 + (n + 1))
                        pe.wait_ge(s_kf[s], b * 2 + n)
                        pe.wait_ge(s_v[s], b * 2 + n)
                        for i in range(2):
                            mm = pe.matmul(p_kv[s][:, i, :], xs[:, s, i * P:(i + 1) * P], wkv[:], start=True, stop=True)
                        mm.then_inc(s_kvp[s], 1)

                    def gather(t):
                        s, n = t % 2, t // 2
                        pe.wait_ge(s_kf[s], b * 2 + (n + 1))
                        pe.wait_ge(s_v[s], b * 2 + (n + 1))
                        if t == 0:
                            pe.wait_ge(s_kv, b * 2)
                        for i in range(2):
                            mm = pe.matmul(p_sum[:], kf[:, s, i, :], v[:, s, i, :],
                                           start=(t == 0 and i == 0), stop=(t == PAIRS - 1 and i == 1))
                        mm.then_inc(s_used[s], 1)

                    project(0)
                    for t in range(PAIRS):
                        if t + 1 < PAIRS:
                            project(t + 1)
                        gather(t)
                    for n in range(2):
                        c = b * 2 + n
                        pe.wait_ge(s_qf, c)
                        pe.matmul(p_q[:], wq[:], g.xT[:, bass.ds(c * CH, CH)], start=True, stop=True).then_inc(s_q, 1)
                        pe.wait_ge(s_qf, c + 1)
                        pe.wait_ge(s_kv, b * 2 + 2)
                        pe.wait_ge(s_mix, c)
                        pe.matmul(p_num[:], kv[:], qf[:], start=True, stop=True)
                        pe.matmul(p_den[:], k1[:], qf[:], start=True, stop=True).then_inc(s_nd, 1)
                        pe.wait_ge(s_mix, c + 1)
                        pe.wait_ge(s_res, c)
                        for i in range(4):
                            mm = pe.matmul(p_y[:, i * D:(i + 1) * D], mixed[:, i * P:(i + 1) * P], wo[:],
                                           start=True, stop=True)
                        mm.then_inc(s_y, 1)

            @block.scalar
            def _(act):
                with act.Fori(0, BATCH) as b:
                    for t in range(PAIRS):
                        s, n = t % 2, t // 2
                        act.wait_ge(s_low[s], b * 2 + (n + 1))
                        if t == 0:
                            act.wait_ge(s_ones, 1)
                        act.wait_ge(s_used[s], b * 2 + n)
                        act.activation(v[:, s, :, 0:D], p_kv[s][:, :, D:2 * D], ACT.Copy).then_inc(s_v[s], 1)
                        act.activation(expd[:, s], low[:, s], ACT.Exp).then_inc(s_exp[s], 1)
                    for n in range(2):
                        act.wait_ge(s_qlow, b * 2 + (n + 1))
                        act.activation(qexp[:], qlow[:], ACT.Exp).then_inc(s_qexp, 1)

            @block.vector
            def _(dve):
                with dve.Fori(0, BATCH) as b:
                    for t in range(PAIRS):
                        s, n = t % 2, t // 2
                        dve.wait_ge(s_kvp[s], b * 2 + (n + 1))
                        dve.wait_ge(s_exp[s], b * 2 + n)
                        dve.tensor_scalar(low[:, s], p_kv[s][:, :, 0:D], 0.0, None, ALU.min).then_inc(s_low[s], 1)
                        dve.wait_ge(s_exp[s], b * 2 + (n + 1))
                        dve.wait_ge(s_v[s], b * 2 + (n + 1))
                        dve.wait_ge(s_used[s], b * 2 + n)
                        dve.scalar_tensor_tensor(out=kf[:, s], in0=p_kv[s][:, :, 0:D], scalar=0.0, in1=expd[:, s],
                                                 op0=ALU.max, op1=ALU.add).then_inc(s_kf[s], 1)
                    for s in range(2):
                        dve.wait_ge(s_used[s], b * 2 + 2)
                    dve.wait_ge(s_nd, b * 2)
                    dve.tensor_tensor(kv[:], p_sum[:, 0:D], same_head[:], ALU.mult).then_inc(s_kv, 1)
                    dve.tensor_scalar(k1[:], same_head[:], p_sum[:, D:D + 1], None, ALU.mult).then_inc(s_kv, 1)
                    for n in range(2):
                        c = b * 2 + n
                        dve.wait_ge(s_q, c + 1)
                        dve.wait_ge(s_qexp, c)
                        dve.tensor_scalar(qlow[:], p_q[:], 0.0, None, ALU.min).then_inc(s_qlow, 1)
                        dve.wait_ge(s_qexp, c + 1)
                        dve.wait_ge(s_nd, c)
                        dve.scalar_tensor_tensor(out=qf[:], in0=p_q[:], scalar=0.0, in1=qexp[:],
                                                 op0=ALU.max, op1=ALU.add).then_inc(s_qf, 1)
                        dve.wait_ge(s_nd, c + 1)
                        dve.tensor_scalar(den[:], p_den[:], 1e-6, None, ALU.add).then_inc(s_eps, 1)
                        dve.wait_ge(s_eps, c + 1)
                        dve.reciprocal(den[:], den[:]).then_inc(s_rec, 1)
                        dve.wait_ge(s_rec, c + 1)
                        dve.wait_ge(s_y, c)
                        dve.tensor_tensor(mixed[:], p_num[:], den[:], ALU.mult).then_inc(s_mix, 1)
                        dve.wait_ge(s_y, c + 1)
                        x = g.x_tok[:, bass.ds(c * 4, 4), :]
                        dve.tensor_tensor(x, p_y[:].rearrange("p (i d) -> p i d", i=4), x, ALU.add).then_inc(s_res, 1)


def lilora(nc, g):
    RANK, DOWN, UP = 4, 100, 50
    with Phase(nc, "lora") as ph:
        down_T = ph.sb("down_T", [DOWN, RANK])
        down_aux = ph.sb("down_aux", [DOWN, D])
        up_T = ph.sb("up_T", [RANK, UP])
        up_auxT = ph.sb("up_auxT", [UP, D])
        base = ph.sb("base", [P, D])
        bias = ph.sb("bias", [1, D])
        inner = ph.sb("inner", [RANK, D])
        outer = ph.sb("outer", [UP, D])
        weight = ph.sb("weight", [P, D])
        xs = ph.sb("xs", [P, 2, CH])
        p_w = [ph.ps(f"w{i}", [P, D]) for i in range(3)]
        p_y = [ph.ps(f"y{i}", [P, CH]) for i in range(2)]
        s_in, s_p, s_w = ph.sem("in"), ph.sem("p"), ph.sem("w")
        s_xs, s_y, s_res = ph.two("xs"), ph.two("y"), ph.two("res")
        with nc.Block() as block:
            @block.sync
            def _(sp):
                for to, of in ((down_T, g.dram["L2_ffn_down_T"]), (down_aux, g.dram["L2_ffn_down_aux"]),
                               (up_T, g.dram["L2_ffn_up_T"]), (up_auxT, g.dram["L2_ffn_up_auxT"]),
                               (base, g.dram["L2_ffn_WT"])):
                    sp.dma_start(to[:], of[:, :]).then_inc(s_in, 16)
                sp.dma_start(bias[:], g.dram["L2_ffn_b"].rearrange("(a d) -> a d", a=1)).then_inc(s_in, 16)
                ph.clear_before(sp)

            @block.scalar
            def _(act):
                with act.Fori(0, NCH // 2) as it:
                    for s in range(2):
                        act.wait_ge(s_y[s], it)
                        act.activation(xs[:, s, :], g.xT[:, bass.ds((it * 2 + s) * CH, CH)], ACT.Copy).then_inc(s_xs[s], 1)

            @block.tensor
            def _(pe):
                pe.wait_ge(s_in, 96)
                pe.matmul(p_w[0][0:RANK, :], down_T[:], down_aux[:], start=True, stop=True).then_inc(s_p, 1)
                pe.wait_ge(s_w, 1)
                pe.matmul(p_w[1][0:UP, :], up_T[:], inner[:], start=True, stop=True).then_inc(s_p, 1)
                pe.wait_ge(s_w, 2)
                pe.matmul(p_w[2][:], outer[:], up_auxT[:], start=True, stop=True).then_inc(s_p, 1)
                pe.wait_ge(s_w, 3)
                with pe.Fori(0, NCH // 2) as it:
                    for s in range(2):
                        pe.wait_ge(s_xs[s], it + 1)
                        pe.wait_ge(s_res[s], it)
                        for i in range(4):
                            y = p_y[s][:, i * D:(i + 1) * D]
                            pe.matmul(y, g.ones[0:1, :], bias[:], start=True, stop=False)
                            mm = pe.matmul(y, xs[:, s, i * P:(i + 1) * P], weight[:], start=False, stop=True)
                        mm.then_inc(s_y[s], 1)

            @block.vector
            def _(dve):
                dve.wait_ge(s_p, 1)
                dve.tensor_copy(inner[:], p_w[0][0:RANK, :]).then_inc(s_w, 1)
                dve.wait_ge(s_p, 2)
                dve.tensor_copy(outer[:], p_w[1][0:UP, :]).then_inc(s_w, 1)
                dve.wait_ge(s_p, 3)
                dve.tensor_tensor(weight[:], p_w[2][:], base[:], ALU.add).then_inc(s_w, 1)
                with dve.Fori(0, NCH // 2) as it:
                    for s in range(2):
                        dve.wait_ge(s_y[s], it + 1)
                        x = g.x_tok[:, bass.ds((it * 2 + s) * 4, 4), :]
                        dve.tensor_tensor(x, p_y[s][:].rearrange("p (i d) -> p i d", i=4), x, ALU.add)\
                           .then_inc(s_res[s], 1)


EXPERTS = 8


def route(nc, g):
    KEEP = 2 * SEQ // EXPERTS
    ROWS = BATCH * EXPERTS
    with Phase(nc, "route") as ph:
        gate_w = ph.sb("gate_w", [P, EXPERTS])
        scoresT = ph.sb("scoresT", [EXPERTS, NT * P])
        top = ph.sb("top", [P, NT])
        shifted = ph.sb("shifted", [P, NT, EXPERTS])
        expd = ph.sb("expd", [P, NT, EXPERTS])
        total = ph.sb("total", [P, NT])
        share = ph.sb("share", [P, NT])
        probs = ph.sb("probs", [P, TB, BATCH, EXPERTS])
        rows = ph.sb("rows", [ROWS, SEQ])
        left = ph.sb("left", [ROWS, SEQ])
        best = ph.sb("best", [ROWS, 8])
        kept = ph.sb("kept", [ROWS, SEQ])
        p_s = [ph.ps(f"s{i}", [EXPERTS, CH]) for i in range(2)]
        p_t = ph.ps("t", [P, NT * EXPERTS])
        p_rows = ph.ps("rows", [ROWS, SEQ])
        p_gate = ph.ps("gate", [P, TB * ROWS])
        s_in, s_turn = ph.sem("in"), ph.sem("turn")
        s_score, s_copied = ph.two("score"), ph.two("copied")
        s_max, s_sub, s_exp, s_sum, s_rec, s_prob = (ph.sem(n) for n in ("max", "sub", "exp", "sum", "rec", "prob"))
        s_rows, s_left, s_best, s_kept, s_back, s_gate = (ph.sem(n) for n in ("rows", "left", "best", "kept", "back", "gate"))
        with nc.Block() as block:
            @block.sync
            def _(sp):
                sp.dma_start(gate_w[:], g.dram["L1_ffn_gate_w"][:, :]).then_inc(s_in, 16)
                ph.clear_before(sp)

            @block.tensor
            def _(pe):
                pe.wait_ge(s_in, 16)
                for c in range(NCH):
                    s = c % 2
                    if c >= 2:
                        pe.wait_ge(s_copied[s], c // 2)
                    pe.matmul(p_s[s][:], gate_w[:], g.xT[:, c * CH:(c + 1) * CH], start=True, stop=True)\
                      .then_inc(s_score[s], 1)
                for s in range(2):
                    pe.wait_ge(s_copied[s], NCH // 2)
                for t in range(NT):
                    mm = pe.transpose(p_t[:, t * EXPERTS:(t + 1) * EXPERTS], scoresT[:, t * P:(t + 1) * P],
                                      g.ident[0:EXPERTS, 0:EXPERTS])
                mm.then_inc(s_turn, 1)
                pe.wait_ge(s_prob, 1)
                for j in range(TB):
                    mm = pe.transpose(p_rows[:, j * P:(j + 1) * P], probs[:, j].rearrange("p n e -> p (n e)"), g.ident[:])
                mm.then_inc(s_rows, 1)
                pe.wait_ge(s_kept, 1)
                for j in range(TB):
                    mm = pe.transpose(p_gate[:, j * ROWS:(j + 1) * ROWS], kept[:, j * P:(j + 1) * P],
                                      g.ident[0:ROWS, 0:ROWS])
                mm.then_inc(s_back, 1)

            @block.scalar
            def _(act):
                for c in range(NCH):
                    act.wait_ge(s_score[c % 2], c // 2 + 1)
                    act.activation(scoresT[:, c * CH:(c + 1) * CH], p_s[c % 2][:], ACT.Copy).then_inc(s_copied[c % 2], 1)
                act.wait_ge(s_sub, 1)
                act.activation(expd[:], shifted[:], ACT.Exp).then_inc(s_exp, 1)

            @block.vector
            def _(dve):
                scores = p_t[:].rearrange("p (t e) -> p t e", e=EXPERTS)
                dve.wait_ge(s_turn, 1)
                dve.tensor_reduce(top[:], scores, AX.X, ALU.max).then_inc(s_max, 1)
                dve.wait_ge(s_max, 1)
                dve.tensor_tensor(shifted[:], scores, across(top[:], EXPERTS), ALU.subtract).then_inc(s_sub, 1)
                dve.wait_ge(s_exp, 1)
                dve.tensor_reduce(total[:], expd[:], AX.X, ALU.add).then_inc(s_sum, 1)
                dve.wait_ge(s_sum, 1)
                dve.reciprocal(share[:], total[:]).then_inc(s_rec, 1)
                dve.wait_ge(s_rec, 1)
                for n in range(BATCH):
                    ins = dve.tensor_tensor(probs[:, :, n, :], expd[:, n * TB:(n + 1) * TB, :],
                                            across(share[:, n * TB:(n + 1) * TB], EXPERTS), ALU.mult)
                ins.then_inc(s_prob, 1)
                dve.wait_ge(s_rows, 1)
                dve.tensor_copy(rows[:], p_rows[:]).then_inc(s_left, 1)
                dve.tensor_copy(left[:], p_rows[:]).then_inc(s_left, 1)
                for n in range(KEEP // 8):
                    dve.wait_ge(s_left, n + 2)
                    dve.max(best[:], left[:]).then_inc(s_best, 1)
                    dve.wait_ge(s_best, n + 1)
                    dve.match_replace(out=left[:], in_to_replace=best[:], in_values=left[:], imm_value=-1.0)\
                       .then_inc(s_left, 1)
                dve.wait_ge(s_left, KEEP // 8 + 2)
                dve.scalar_tensor_tensor(out=kept[:], in0=left[:], scalar=0.0, in1=rows[:],
                                         op0=ALU.is_lt, op1=ALU.mult).then_inc(s_kept, 1)
                dve.wait_ge(s_back, 1)
                for n in range(BATCH):
                    dve.tensor_copy(g.gates[:, n * TB:(n + 1) * TB, :],
                                    p_gate[:].rearrange("p (j n e) -> p j n e", j=TB, n=BATCH)[:, :, n, :])\
                       .then_inc(s_gate, 1)


def experts(nc, g):
    HID = 512
    HT = HID // P
    with Phase(nc, "exp") as ph:
        w1 = ph.sb("w1", [P, EXPERTS, HID])
        w2 = ph.sb("w2", [P, EXPERTS, HT, D])
        hidden = ph.sb("hidden", [P, 2, HT, CH])
        acc = ph.sb("acc", [P, 4, D])
        rounded = ph.sb("rounded", [P, 4, D], BF16)
        hid = [ph.ps(f"hid{j}", [P, CH]) for j in range(HT)]
        out = [ph.ps(f"out{i}", [P, CH]) for i in range(2)]
        s_w = ph.sem("w")
        s_hid, s_gelu, s_acc, s_round, s_res = (ph.sem(n) for n in ("hid", "gelu", "acc", "round", "res"))
        s_out = ph.two("out")
        with nc.Block() as block:
            @block.sync
            def _(sp):
                sp.dma_start(w1[:], g.dram["L1_ffn_w1"].rearrange("e d f -> d e f")).then_inc(s_w, 16)
                sp.dma_start(w2[:].rearrange("p e j d -> p (e j) d"),
                             g.dram["L1_ffn_w2"].rearrange("e (j p) d -> p (e j) d", p=P)).then_inc(s_w, 16)
                ph.clear_before(sp)

            @block.tensor
            def _(pe):
                pe.wait_ge(s_w, 32)
                with pe.Fori(0, NCH) as c:
                    def up(e):
                        for j in range(HT):
                            if e:
                                pe.wait_ge(s_gelu, c * (EXPERTS * HT) + ((e - 1) * HT + j + 1))
                            pe.matmul(hid[j][:], w1[:, e, j * P:(j + 1) * P], g.xT[:, bass.ds(c * CH, CH)],
                                      start=True, stop=True).then_inc(s_hid, 1)

                    def down(e):
                        s = e % 2
                        pe.wait_ge(s_gelu, c * (EXPERTS * HT) + (e + 1) * HT)
                        if e > 1:
                            pe.wait_ge(s_acc, c * EXPERTS + (e - 1))
                        else:
                            pe.wait_ge(s_acc, c * EXPERTS)
                        for i in range(4):
                            for j in range(HT):
                                mm = pe.matmul(out[s][:, i * D:(i + 1) * D], hidden[:, s, j, i * P:(i + 1) * P],
                                               w2[:, e, j, :], start=(j == 0), stop=(j == HT - 1))
                        mm.then_inc(s_out[s], 1)

                    up(0)
                    for e in range(EXPERTS):
                        if e + 1 < EXPERTS:
                            up(e + 1)
                        down(e)

            @block.scalar
            def _(act):
                with act.Fori(0, NCH) as c:
                    for e in range(EXPERTS):
                        s = e % 2
                        for j in range(HT):
                            act.wait_ge(s_hid, c * (EXPERTS * HT) + (e * HT + j + 1))
                            if j == 0:
                                act.wait_ge(s_out[s], c * (EXPERTS // 2) + e // 2)
                            act.activation(hidden[:, s, j, :], hid[j][:], ACT.Gelu_apprx_tanh).then_inc(s_gelu, 1)

            @block.vector
            def _(dve):
                with dve.Fori(0, NCH) as c:
                    for e in range(EXPERTS):
                        s = e % 2
                        dve.wait_ge(s_out[s], c * (EXPERTS // 2) + (e // 2 + 1))
                        if e:
                            dve.wait_ge(s_acc, c * EXPERTS + e)
                        else:
                            dve.wait_ge(s_round, c)
                        for i in range(4):
                            y = out[s][:, i * D:(i + 1) * D]
                            weight = g.gates[:, bass.ds(c * 4 + i, 1), e]
                            if e:
                                ins = dve.scalar_tensor_tensor(out=acc[:, i, :], in0=y, scalar=weight, in1=acc[:, i, :],
                                                               op0=ALU.mult, op1=ALU.add)
                            else:
                                ins = dve.tensor_scalar(acc[:, i, :], y, weight, None, ALU.mult)
                        ins.then_inc(s_acc, 1)
                    dve.wait_ge(s_acc, (c + 1) * EXPERTS)
                    dve.wait_ge(s_res, c)
                    dve.tensor_copy(rounded[:], acc[:]).then_inc(s_round, 1)
                    dve.wait_ge(s_round, c + 1)
                    x = g.x_tok[:, bass.ds(c * 4, 4), :]
                    dve.tensor_tensor(x, rounded[:], x, ALU.add).then_inc(s_res, 1)


def multilevel_attention(nc, g):
    HEADS, DH, GROUPS, HG = 16, 8, 4, 4
    PREV = 64
    EXTRA = PREV + 16 + 3 * 8
    KEYS = P + EXTRA
    VW = DH + 1
    STEPS = 4
    SCALE = DH ** -0.5
    with Phase(nc, "mla") as ph:
        wq = ph.sb("wq", [P, GROUPS * P])
        wk = ph.sb("wk", [P, GROUPS * P])
        wv = ph.sb("wv", [P, D])
        wproj = ph.sb("wproj", [P, D])
        bq = ph.sb("bq", [P, GROUPS])
        bk_row = ph.sb("bk_row", [1, GROUPS * P])
        bv_row = ph.sb("bv_row", [1, D])
        bproj = ph.sb("bproj", [1, D])
        there = ph.sb("there", [1, TB * KEYS])
        there_sum = ph.sb("there_sum", [1, TB * EXTRA])
        there_col = ph.sb("there_col", [1, 2, EXTRA])
        mean_of = ph.sb("mean_of", [P, EXTRA])
        count = ph.sb("count", [EXTRA, 1])
        maskadd = ph.sb("maskadd", [P, 2 * KEYS])
        mask16 = ph.sb("mask16", [P, 2 * KEYS], BF16)
        ident16 = ph.sb("ident16", [P, P], BF16)
        xk = ph.sb("xk", [P, 2, KEYS])
        xv = ph.sb("xv", [P, 2, EXTRA])
        by8 = ph.sb("by8", [P, 128])
        by16 = ph.sb("by16", [P, 64])
        by32 = ph.sb("by32", [P, 32])
        by64 = ph.sb("by64", [P, 16])
        xsum = ph.sb("xsum", [P, TB, EXTRA])
        xmean = ph.sb("xmean", [P, TB, EXTRA])
        k = ph.sb("k", [P, 2, GROUPS, KEYS])
        v_own = ph.sb("v_own", [P, 2, HEADS, VW])
        v_extra = ph.sb("v_extra", [EXTRA, 2, HEADS, VW])
        q = ph.sb("q", [P, 2, GROUPS, P])
        top = ph.sb("top", [P, 2, GROUPS, 5])
        nmin = ph.sb("nmin", [P, 2, GROUPS])
        probs = ph.sb("probs", [P, 2, GROUPS, KEYS])
        pT = ph.sb("pT", [P, 2, 2, GROUPS * P])
        share = ph.sb("share", [P, 2, HEADS])
        ctx_ = ph.sb("ctx", [P, 2, D])
        ctxT = ph.sb("ctxT", [P, 2, D])
        p_s = [ph.ps(f"s{i}", [P, CH]) for i in range(4)]
        p_t = [ph.ps(f"t{i}", [P, CH]) for i in range(2)]
        p_o = ph.ps("o", [P, HEADS * VW])
        p_y = ph.ps("y", [P, CH])
        s_in, s_one, s_mask = ph.sem("in"), ph.sem("one"), ph.sem("mask")
        s_xs, s_pool, s_xe = ph.sem("xs"), ph.sem("pool"), ph.sem("xe")
        s_k, s_kc, s_v, s_vc = ph.sem("k"), ph.sem("kc"), ph.sem("v"), ph.sem("vc")
        s_q, s_qs, s_s, s_top, s_min, s_neg, s_exp = (ph.sem(n) for n in ("q", "qs", "s", "top", "min", "neg", "exp"))
        s_t, s_ta, s_td, s_o, s_share, s_ctx, s_ct, s_ctc, s_y, s_res = (
            ph.sem(n) for n in ("t", "ta", "td", "o", "share", "ctx", "ct", "ctc", "y", "res"))
        with nc.Block() as block:
            @block.sync
            def _(sp):
                for to, of in ((wq[:], g.dram["L2_attn_wq"]), (wk[:], g.dram["L2_attn_wk"]), (wv[:], g.dram["L2_attn_wv"]),
                               (wproj[:], g.dram["L2_attn_W_proj"]), (bq[:], g.dram["L2_attn_bq"]), 
                               (bk_row[:], g.dram["L2_attn_bk_row"]), (bv_row[:], g.dram["L2_attn_bv_row"]),
                               (bproj[:], g.dram["L2_attn_bproj"]), (there[:], g.dram["c_there"]),
                               (there_sum[:], g.dram["c_there_sum"]), (mean_of[:], g.dram["c_mean_of"]),
                               (count[:], g.dram["c_count"]), (maskadd[:], g.dram["c_band64"])):
                    sp.dma_start(to, of[:, :]).then_inc(s_in, 16)
                ph.clear_before(sp)

            @block.gpsimd
            def _(pool):
                pool.memset(v_own[:], 1.0).then_inc(s_one, 1)
                pool.memset(xsum[:], 0.0).then_inc(s_one, 1)
                pool.wait_ge(s_in, 13 * 16)
                with pool.Fori(0, BATCH) as b:
                    with pool.Fori(0, TB // 2) as jj:
                        for u in range(2):
                            pool.wait_ge(s_xe, b + 1)
                            pool.wait_ge(s_v, b * TB + jj * 2)
                            pool.tensor_copy(xk[:, u, 0:P], g.xT[:, bass.ds((b * TB + jj * 2 + u) * P, P)])
                            pool.tensor_copy(xk[:, u, P:KEYS], xmean[:, bass.ds(jj * 2 + u, 1), :].rearrange("p a e -> p (a e)"))
                            pool.tensor_copy(there_col[:, u, :], there_sum[:, bass.ds((jj * 2 + u) * EXTRA, EXTRA)])
                            pool.tensor_copy(xv[:, u, :], xsum[:, bass.ds(jj * 2 + u, 1), :].rearrange("p a e -> p (a e)"))\
                                .then_inc(s_xs, 1)

            @block.tensor
            def _(pe):
                pe.wait_ge(s_in, 13 * 16)
                pe.wait_ge(s_mask, 2)

                with pe.Fori(0, BATCH) as b:
                    with pe.Fori(0, TB // 2) as jj:
                        def tile(u):
                            return b * TB + jj * 2 + u

                        def query(u):
                            pe.wait_ge(s_xs, tile(u) + 1)
                            pe.wait_ge(s_res, tile(u)) if u == 0 else pe.wait_ge(s_qs, tile(0) + 1)
                            for group in range(GROUPS):
                                mm = pe.matmul(p_y[:, group * P:(group + 1) * P], wq[:, group * P:(group + 1) * P],
                                               xk[:, u, 0:P], start=True, stop=True)
                            mm.then_inc(s_q, 1)

                        def keys(u):
                            pe.wait_ge(s_exp, tile(0) * STEPS)
                            for group in range(GROUPS):
                                to = p_s[2 * u + group // 2][:, (group % 2) * KEYS:(group % 2 + 1) * KEYS]
                                cols = slice(group * P, (group + 1) * P)
                                pe.matmul(to, wk[:, cols], xk[:, u, :], start=True, stop=False)
                                mm = pe.matmul(to, bk_row[:, cols], there[:, bass.ds((jj * 2 + u) * KEYS, KEYS)],
                                               start=False, stop=True)
                            mm.then_inc(s_k, 1)
                            pe.wait_ge(s_ta, tile(0) * STEPS)
                            pe.wait_ge(s_td, tile(0) * STEPS)
                            pe.matmul(p_t[u][:, 0:D], g.ones[0:1, :], bv_row[:], start=True, stop=False)
                            pe.matmul(p_t[u][:, 0:D], xk[:, u, 0:P], wv[:], start=False, stop=True)
                            pe.matmul(p_t[u][0:EXTRA, D:2 * D], xv[:, u, :], wv[:], start=True, stop=False)
                            pe.matmul(p_t[u][0:EXTRA, D:2 * D], there_col[:, u, :], bv_row[:], start=False, stop=True)\
                              .then_inc(s_v, 1)

                        def scores(n):
                            u, h = n // STEPS, n % STEPS
                            step = tile(0) * STEPS + n
                            if h == 0:
                                pe.wait_ge(s_qs, tile(u) + 1)
                                pe.wait_ge(s_kc, tile(1) + 1)
                            if n >= 2:
                                pe.wait_ge(s_exp, step - 1)
                            rows = slice(32 * h, 32 * h + DH)
                            for group in range(GROUPS):
                                bank = p_s[2 * (n % 2) + group // 2]
                                at = (group % 2) * KEYS
                                if group % 2 == 0:
                                    pe.matmul(bank[:, 0:2 * KEYS], ident16[:], mask16[:], start=True, stop=False)
                                last = group % 2 == 1
                                mm = pe.matmul(bank[:, at:at + KEYS], q[rows, u, group, :], k[rows, u, group, :],
                                               start=False, stop=last)
                            mm.then_inc(s_s, 1)

                        def turn(n):
                            step = tile(0) * STEPS + n
                            pe.wait_ge(s_exp, step + 1)
                            pe.wait_ge(s_ta, step)
                            pe.wait_ge(s_td, step)
                            if n == 0:
                                pe.wait_ge(s_vc, tile(1) + 1)
                            for group in range(GROUPS):
                                pe.transpose(p_t[0][:, group * P:(group + 1) * P], probs[:, n % 2, group, 0:P], g.ident[:])
                            for group in range(GROUPS):
                                mm = pe.transpose(p_t[1][0:EXTRA, group * P:(group + 1) * P],
                                                  probs[:, n % 2, group, P:KEYS], g.ident[:])
                            mm.then_inc(s_t, 1)

                        def values(n):
                            u, h = n // STEPS, n % STEPS
                            step = tile(0) * STEPS + n
                            pe.wait_ge(s_ta, step + 1)
                            pe.wait_ge(s_td, step + 1)
                            if h == 0:
                                pe.wait_ge(s_ctx, tile(u))
                            for group in range(GROUPS):
                                head = group * HG + h
                                out = p_o[:, head * VW:(head + 1) * VW]
                                cols = slice(group * P, (group + 1) * P)
                                pe.matmul(out, pT[:, n % 2, 0, cols],
                                          v_own[:, u, head, :], start=True, stop=False)
                                mm = pe.matmul(out, pT[0:EXTRA, n % 2, 1, cols],
                                               v_extra[:, u, head, :], start=False, stop=True)
                            mm.then_inc(s_o, 1)

                        def out_project(u):
                            pe.wait_ge(s_ctx, tile(u) + 1)
                            pe.wait_ge(s_qs, tile(1) + 1)
                            if u:
                                pe.wait_ge(s_res, tile(u))
                            pe.transpose(p_y[:, 0:P], ctx_[:, u, :], g.ident[:]).then_inc(s_ct, 1)
                            pe.wait_ge(s_ctc, tile(u) + 1)
                            pe.matmul(p_y[:, 0:D], g.ones[0:1, :], bproj[:], start=True, stop=False)
                            pe.matmul(p_y[:, 0:D], ctxT[:, u, :], wproj[:], start=False, stop=True).then_inc(s_y, 1)

                        query(0)
                        keys(0)
                        query(1)
                        keys(1)
                        scores(0)
                        for n in range(2 * STEPS):
                            if n + 1 < 2 * STEPS:
                                scores(n + 1)
                            turn(n)
                            if n:
                                values(n - 1)
                            if n == STEPS + 1:
                                out_project(0)
                        values(2 * STEPS - 1)
                        out_project(1)

            @block.scalar
            def _(act):
                act.wait_ge(s_one, 1)
                with act.Fori(0, BATCH) as b:
                    with act.Fori(0, TB // 2) as jj:
                        for u in range(2):
                            act.wait_ge(s_k, b * TB + jj * 2 + (u + 1))
                            for half in range(2):
                                ins = act.activation(k[:, u, 2 * half:2 * half + 2, :].rearrange("p a e -> p (a e)"),
                                                     p_s[2 * u + half][:, 0:2 * KEYS], ACT.Copy)
                            ins.then_inc(s_kc, 1)
                        for n in range(2 * STEPS + 1):
                            if n < 2 * STEPS:
                                step = (b * TB + jj * 2) * STEPS + n
                                act.wait_ge(s_neg, step + 1)
                                if n >= 2:
                                    act.wait_ge(s_t, step - 1)
                                else:
                                    act.wait_ge(s_t, (b * TB + jj * 2) * STEPS)
                                for group in range(GROUPS):
                                    bank = p_s[2 * (n % 2) + group // 2]
                                    at = (group % 2) * KEYS
                                    ins = act.activation(probs[:, n % 2, group, :], bank[:, at:at + KEYS], ACT.Exp,
                                                         bias=nmin[:, n % 2, group:group + 1])
                                ins.then_inc(s_exp, 1)
                            if n >= 1:
                                step = (b * TB + jj * 2) * STEPS + (n - 1)
                                act.wait_ge(s_t, step + 1)
                                if n >= 3:
                                    act.wait_ge(s_o, step - 1)
                                else:
                                    act.wait_ge(s_o, (b * TB + jj * 2) * STEPS)
                                act.activation(pT[:, (n - 1) % 2, 0, :], p_t[0][:], ACT.Copy).then_inc(s_ta, 1)
                            if n == STEPS + 2 or n == 2 * STEPS:
                                u = 0 if n == STEPS + 2 else 1
                                act.wait_ge(s_ct, b * TB + jj * 2 + (u + 1))
                                act.activation(ctxT[:, u, :], p_y[:, 0:P], ACT.Copy).then_inc(s_ctc, 1)

            @block.vector
            def _(dve):
                dve.wait_ge(s_in, 13 * 16)
                dve.wait_ge(s_one, 2)
                dve.tensor_copy(mask16[:], maskadd[:]).then_inc(s_mask, 1)
                dve.tensor_copy(ident16[:], g.ident[:]).then_inc(s_mask, 1)
                dve.tensor_copy(v_extra[:].rearrange("p j h d -> p (j h d)"),
                                count[:].to_broadcast([EXTRA, 2 * HEADS * VW])).then_inc(s_mask, 1)
                dve.wait_ge(s_mask, 3)

                def pooled(b):
                    dve.wait_ge(s_xs, b * TB)
                    x = g.xT[:, bass.ds(b * SEQ, SEQ)]
                    dve.tensor_reduce(by8[:], x.rearrange("p (a s) -> p a s", s=8), AX.X, ALU.add).then_inc(s_pool, 1)
                    for n, (of, to) in enumerate(((by8, by16), (by16, by32), (by32, by64))):
                        dve.wait_ge(s_pool, b * 5 + (n + 1))
                        dve.tensor_reduce(to[:], of[:].rearrange("p (a s) -> p a s", s=2), AX.X, ALU.add).then_inc(s_pool, 1)
                    dve.tensor_copy(xsum[:, 1:TB, 0:PREV],
                                    g.xT[:, bass.ds(b * SEQ + PREV, (TB - 1) * P)].rearrange("p (j k) -> p j k", k=P)[:, :, 0:PREV])
                    dve.tensor_copy(xsum[:, 1:TB, PREV:PREV + 16], by8[:, 8:120].rearrange("p (j k) -> p j k", k=16))
                    dve.tensor_copy(xsum[:, 0, PREV + 8:PREV + 16], by8[:, 0:8])
                    dve.wait_ge(s_pool, b * 5 + 4)
                    dve.tensor_copy(xsum[:, 1:TB, PREV + 16:PREV + 24], by16[:, 0:56].rearrange("p (j k) -> p j k", k=8))
                    for u in range(2):
                        dve.tensor_copy(xsum[:, 2 + u:TB:2, PREV + 24:PREV + 32], by32[:, 0:24].rearrange("p (j k) -> p j k", k=8))
                    dve.tensor_copy(xsum[:, 4:TB, PREV + 32:PREV + 40],
                                    by64[:, 0:8].unsqueeze(1).to_broadcast([P, 4, 8])).then_inc(s_pool, 1)
                    dve.wait_ge(s_pool, b * 5 + 5)
                    dve.tensor_tensor(xmean[:], xsum[:], mean_of[:].unsqueeze(1).to_broadcast([P, TB, EXTRA]), ALU.mult)\
                       .then_inc(s_xe, 1)

                with dve.Fori(0, BATCH) as b:
                    pooled(b)
                    with dve.Fori(0, TB // 2) as jj:
                        def tile(u):
                            return b * TB + jj * 2 + u

                        def query(u):
                            dve.wait_ge(s_q, tile(u) + 1)
                            for group in range(GROUPS):
                                ins = dve.tensor_scalar(q[:, u, group, :], p_y[:, group * P:(group + 1) * P],
                                                        bq[:, group:group + 1], SCALE, ALU.add, ALU.mult)
                            ins.then_inc(s_qs, 1)

                        def values(u):
                            dve.wait_ge(s_v, tile(u) + 1)
                            dve.tensor_copy(v_own[:, u, :, 0:DH], p_t[u][:, 0:D].rearrange("p (h d) -> p h d", d=DH))
                            dve.tensor_copy(v_extra[:, u, :, 0:DH],
                                            p_t[u][0:EXTRA, D:2 * D].rearrange("p (h d) -> p h d", d=DH)).then_inc(s_vc, 1)

                        def maxima(n):
                            s = n % 2
                            step = tile(0) * STEPS + n
                            dve.wait_ge(s_s, step + 1)
                            if n >= 2:
                                dve.wait_ge(s_exp, step - 1)
                            for pair in range(2):
                                view = p_s[2 * s + pair][:, 0:2 * KEYS].rearrange("p (a k) -> p a k", k=KEYS)
                                to = top[:, s, 2 * pair:2 * pair + 2, :]
                                dve.tensor_reduce(to[:, :, 0:1], view[:, :, 0:P + PREV], AX.X, ALU.max)
                                dve.tensor_reduce(to[:, :, 1:2], view[:, :, P + PREV:P + PREV + 16], AX.X, ALU.max)
                                ins = dve.tensor_reduce(to[:, :, 2:5],
                                                        view[:, :, P + PREV + 16:KEYS].rearrange("p a (l k) -> p a l k", k=8),
                                                        AX.X, ALU.max)
                            ins.then_inc(s_top, 1)
                            dve.wait_ge(s_top, step + 1)
                            dve.tensor_reduce(nmin[:, s, :], top[:, s], AX.X, ALU.min).then_inc(s_min, 1)
                            dve.wait_ge(s_min, step + 1)
                            dve.tensor_scalar(nmin[:, s, :], nmin[:, s, :], -1.0, None, ALU.mult).then_inc(s_neg, 1)

                        def turned(n):
                            step = tile(0) * STEPS + n
                            dve.wait_ge(s_t, step + 1)
                            if n >= 2:
                                dve.wait_ge(s_o, step - 1)
                            else:
                                dve.wait_ge(s_o, tile(0) * STEPS)
                            dve.tensor_copy(pT[0:EXTRA, n % 2, 1, :], p_t[1][0:EXTRA, :]).then_inc(s_td, 1)

                        def context(u):
                            o = p_o[:].rearrange("p (h w) -> p h w", w=VW)
                            dve.wait_ge(s_o, (tile(u) + 1) * STEPS)
                            dve.reciprocal(share[:, u, :], o[:, :, DH]).then_inc(s_share, 1)
                            dve.wait_ge(s_share, tile(u) + 1)
                            dve.tensor_tensor(ctx_[:, u, :].rearrange("p (h d) -> p h d", d=DH), o[:, :, 0:DH],
                                              across(share[:, u, :], DH), ALU.mult).then_inc(s_ctx, 1)

                        def result(u):
                            dve.wait_ge(s_y, tile(u) + 1)
                            x = g.x_tok[:, bass.ds(tile(u), 1), :].rearrange("p a d -> p (a d)")
                            dve.tensor_tensor(x, p_y[:, 0:D], x, ALU.add).then_inc(s_res, 1)

                        query(0)
                        values(0)
                        query(1)
                        values(1)
                        maxima(0)
                        for n in range(2 * STEPS):
                            if n + 1 < 2 * STEPS:
                                maxima(n + 1)
                            turned(n)
                            if n == STEPS:
                                context(0)
                            if n == STEPS + 1:
                                result(0)
                        context(1)
                        result(1)


def hedgehog(nc, g):
    HEADS, DV, GROUPS, HG = 8, 16, 2, 4
    DF = 2 * DV
    GV = HG * DV
    SCALE = DF ** -0.5
    with Phase(nc, "hh") as ph:
        wqk = ph.sb("wqk", [P, 2, D])
        feature_w = ph.sb("feature_w", [P, 2, GROUPS * P])
        w = ph.sb("w", [P, 2, GROUPS * P])
        wvT = ph.sb("wvT", [P, D])
        woT = ph.sb("woT", [P, D])
        rms_w = ph.sb("rms_w", [P, 1])
        bias = ph.sb("bias", [P, 2])
        sign = ph.sb("sign", [P, 1])
        causal = ph.sb("causal", [P, P])
        own_head = ph.sb("own_head", [P, GV])
        xs = ph.sb("xs", [P, 2, CH])
        feat = ph.sb("feat", [P, 2, 2 * GROUPS, CH])
        vf = ph.sb("vf", [P, 2, D + GROUPS * P])
        attn = ph.sb("attn", [P, 2, HG, 2 * GROUPS, P])
        state = ph.sb("state", [P, GROUPS, GV])
        update = ph.sb("update", [P, GROUPS, GV])
        o = ph.sb("o", [P, 2, CH])
        osq = ph.sb("osq", [P, 2, CH])
        power = ph.sb("power", [P, 2, CH // DV])
        var = ph.sb("var", [P, 2, CH // DV])
        rstd = ph.sb("rstd", [P, 2, CH // DV])
        on = ph.sb("on", [P, 2, CH])
        oT = ph.sb("oT", [P, 2, CH])
        p_a = [ph.ps(f"a{i}", [P, CH]) for i in range(HG)]
        p_m = ph.ps("m", [P, D + GROUPS * P])
        p_o = ph.ps("o", [P, D])
        p_s = ph.ps("s", [P, GROUPS * GV])
        p_y = ph.ps("y", [P, CH])
        s_in, s_w, s_wc, s_bias = ph.sem("in"), ph.sem("w"), ph.sem("wc"), ph.sem("bias")
        s_feat, s_exp, s_xs = ph.sem("feat"), ph.sem("exp"), ph.sem("xs")
        s_m, s_vf, s_tile = ph.sem("m"), ph.sem("vf"), ph.two("tile")
        s_att, s_mask = ([ph.sem(f"{n}{h}") for h in range(HG)] for n in ("att", "mask"))
        s_o, s_oc, s_sraw, s_upd, s_state = (ph.sem(n) for n in ("o", "oc", "sraw", "upd", "state"))
        s_sq, s_pow, s_var, s_rstd, s_on, s_ot, s_otc, s_y, s_res = (
            ph.sem(n) for n in ("sq", "pow", "var", "rstd", "on", "ot", "otc", "y", "res"))
        STEPS = TB + 1
        with nc.Block() as block:
            @block.sync
            def _(sp):
                for to, of in ((wqk[:, 0], g.dram["L3_attn_Wq"]), (wqk[:, 1], g.dram["L3_attn_Wk"]),
                               (feature_w[:, 0], g.dram["L3_attn_fq"]), (feature_w[:, 1], g.dram["L3_attn_fk"]),
                               (wvT[:], g.dram["L3_attn_WvT"]), (woT[:], g.dram["L3_attn_WoT"]),
                               (rms_w[:], g.dram["L3_attn_rms"]), (bias[:], g.dram["L3_attn_fb"]),
                               (sign[:], g.dram["c_sign"]), (causal[:], g.dram["c_causal"]), (own_head[:], g.dram["c_own_head"])):
                    sp.dma_start(to, of[:, :]).then_inc(s_in, 16)
                ph.clear_before(sp)

            @block.gpsimd
            def _(pool):
                with pool.Fori(0, BATCH) as b:
                    for n in range(2):
                        c = b * 2 + n
                        pool.wait_ge(s_tile[n], b * 4)
                        pool.tensor_copy(xs[:, n, :], g.xT[:, bass.ds(c * CH, CH)]).then_inc(s_xs, 1)
                    for n in range(2):
                        c = b * 2 + n
                        pool.wait_ge(s_oc, c * 4 + 4)
                        pool.tensor_tensor(osq[:, n], o[:, n], o[:, n], ALU.mult).then_inc(s_sq, 1)
                        pool.wait_ge(s_var, c + 1)
                        pool.tensor_tensor(rstd[:, n], var[:, n], g.minus_half[:, 0:CH // DV], ALU.pow).then_inc(s_rstd, 1)

            @block.scalar
            def _(act):
                act.wait_ge(s_bias, 2)
                with act.Fori(0, BATCH) as b:
                    def tail(n):
                        c = b * 2 + n
                        act.wait_ge(s_ot, c + 1)
                        act.activation(oT[:, n], p_y[:], ACT.Copy).then_inc(s_otc, 1)

                    for n in range(2):
                        c = b * 2 + n
                        act.wait_ge(s_tile[n], b * 4)
                        for f in range(2 * GROUPS):
                            act.wait_ge(s_feat, c * 4 + (f + 1))
                            kind = f // GROUPS
                            act.activation(feat[:, n, f, :], p_a[f][:], ACT.Exp, bias=bias[:, kind:kind + 1],
                                           scale=sign[:, 0:1]).then_inc(s_exp, 1)
                        act.wait_ge(s_sq, c)
                        act.wait_ge(s_on, c)
                        for i in range(4):
                            act.wait_ge(s_o, c * 4 + (i + 1))
                            act.activation(o[:, n, i * D:(i + 1) * D], p_o[:], ACT.Copy, scale=SCALE).then_inc(s_oc, 1)
                            if n == 1 and i == 1:
                                tail(0)
                    tail(1)

            @block.tensor
            def _(pe):
                pe.wait_ge(s_in, 176)
                for k in range(2):
                    pe.matmul(p_a[k][:, 0:GROUPS * P], wqk[:, k], feature_w[:, k], start=True, stop=True).then_inc(s_w, 1)
                pe.wait_ge(s_wc, 3)
                with pe.Fori(0, BATCH) as b:
                    def features(n):
                        c = b * 2 + n
                        for f in range(2 * GROUPS):
                            pe.wait_ge(s_mask[f], c * 2)
                            kind, group = f // GROUPS, f % GROUPS
                            pe.matmul(p_a[f][:], w[:, kind, group * P:(group + 1) * P], g.xT[:, bass.ds(c * CH, CH)],
                                      start=True, stop=True).then_inc(s_feat, 1)

                    def values(n, i):
                        t = b * TB + (4 * n + i)
                        pe.wait_ge(s_vf, t)
                        if i == 0:
                            pe.wait_ge(s_xs, b * 2 + (n + 1))
                            pe.wait_ge(s_exp, b * 8 + (4 * n + 4))
                        pe.matmul(p_m[:, 0:D], xs[:, n, i * P:(i + 1) * P], wvT[:], start=True, stop=True)
                        for group in range(GROUPS):
                            mm = pe.transpose(p_m[:, D + group * P:D + (group + 1) * P],
                                              feat[:, n, GROUPS + group, i * P:(i + 1) * P], g.ident[:])
                        mm.then_inc(s_m, 1)

                    def scores(n, pair):
                        for h in range(HG):
                            pe.wait_ge(s_mask[h], b * 4 + (2 * n + pair))
                            rows = slice(DF * h, DF * h + DF)
                            for u in range(2):
                                cols = slice((2 * pair + u) * P, (2 * pair + u + 1) * P)
                                for group in range(GROUPS):
                                    at = (u * GROUPS + group) * P
                                    mm = pe.matmul(p_a[h][:, at:at + P], feat[rows, n, GROUPS + group, cols],
                                                   feat[rows, n, group, cols], start=True, stop=True)
                            mm.then_inc(s_att[h], 1)

                    def mix(n, i):
                        t = b * TB + (4 * n + i)
                        pair, u = i // 2, i % 2
                        pe.wait_ge(s_vf, t + 1)
                        pe.wait_ge(s_state, b * STEPS + (4 * n + i + 1))
                        if u == 0:
                            for h in range(HG):
                                pe.wait_ge(s_mask[h], b * 4 + (2 * n + pair + 1))
                        pe.wait_ge(s_oc, t)
                        for group in range(GROUPS):
                            out = p_o[:, group * GV:(group + 1) * GV]
                            pe.matmul(out, feat[:, n, group, i * P:(i + 1) * P], state[:, group, :], start=True, stop=False)
                            for h in range(HG):
                                col = group * GV + h * DV
                                mm = pe.matmul(p_o[:, col:col + DV], attn[:, pair, h, u * GROUPS + group, :],
                                               vf[:, i % 2, col:col + DV], start=False, stop=(h == HG - 1))
                        mm.then_inc(s_o, 1)
                        for group in range(GROUPS):
                            at = D + group * P
                            mm = pe.matmul(p_s[:, group * GV:(group + 1) * GV], vf[:, i % 2, at:at + P],
                                           vf[:, i % 2, group * GV:(group + 1) * GV], start=True, stop=True)
                        mm.then_inc(s_sraw, 1)
                        pe.wait_ge(s_sraw, t + 1)
                        pe.sem_inc(s_tile[n], 1)

                    def tail(n):
                        c = b * 2 + n
                        pe.wait_ge(s_on, c + 1)
                        pe.wait_ge(s_res, c)
                        for i in range(4):
                            mm = pe.transpose(p_y[:, i * P:(i + 1) * P], on[:, n, i * D:(i + 1) * D], g.ident[:])
                        mm.then_inc(s_ot, 1)
                        pe.wait_ge(s_otc, c + 1)
                        for i in range(4):
                            mm = pe.matmul(p_y[:, i * D:(i + 1) * D], oT[:, n, i * P:(i + 1) * P], woT[:],
                                           start=True, stop=True)
                        mm.then_inc(s_y, 1)

                    for n in range(2):
                        features(n)
                        values(n, 0)
                        for pair in range(2):
                            scores(n, pair)
                            values(n, 2 * pair + 1)
                            mix(n, 2 * pair)
                            if pair == 0:
                                values(n, 2)
                            mix(n, 2 * pair + 1)
                            if n == 1 and pair == 0:
                                tail(0)
                    tail(1)

            @block.vector
            def _(dve):
                dve.wait_ge(s_in, 176)
                dve.tensor_scalar(bias[:], bias[:], sign[:, 0:1], None, ALU.mult).then_inc(s_bias, 2)
                dve.tensor_scalar(woT[:], woT[:], rms_w[:, 0:1], None, ALU.mult).then_inc(s_wc, 1)
                for k in range(2):
                    dve.wait_ge(s_w, k + 1)
                    dve.tensor_copy(w[:, k], p_a[k][:, 0:GROUPS * P]).then_inc(s_wc, 1)
                with dve.Fori(0, BATCH) as b:
                    def values(n, i):
                        t = b * TB + (4 * n + i)
                        dve.wait_ge(s_m, t + 1)
                        if i < 2:
                            if n:
                                dve.wait_ge(s_sraw, b * TB + (4 * n + i - 1))
                            else:
                                dve.wait_ge(s_sraw, b * TB)
                        else:
                            dve.wait_ge(s_sraw, b * TB + (4 * n + i - 1))
                        dve.tensor_copy(vf[:, i % 2], p_m[:]).then_inc(s_vf, 1)

                    def mask(n, pair):
                        for h in range(HG):
                            dve.wait_ge(s_att[h], b * 4 + (2 * n + pair + 1))
                            dve.tensor_tensor(attn[:, pair, h], p_a[h][:].rearrange("p (a q) -> p a q", q=P),
                                              causal[:].unsqueeze(1).to_broadcast([P, 2 * GROUPS, P]), ALU.mult)\
                               .then_inc(s_mask[h], 1)

                    def update_state(n, i):
                        t = b * TB + (4 * n + i)
                        dve.wait_ge(s_sraw, t + 1)
                        dve.tensor_tensor(update[:], p_s[:].rearrange("p (a v) -> p a v", a=GROUPS),
                                          own_head[:].unsqueeze(1).to_broadcast([P, GROUPS, GV]), ALU.mult).then_inc(s_upd, 1)
                        dve.wait_ge(s_upd, t + 1)
                        dve.tensor_tensor(state[:], state[:], update[:], ALU.add).then_inc(s_state, 1)
                        dve.wait_ge(s_state, b * STEPS + (4 * n + i + 2))

                    def norm(n):
                        c = b * 2 + n
                        dve.wait_ge(s_sq, c + 1)
                        dve.tensor_reduce(power[:, n], osq[:, n].rearrange("p (a v) -> p a v", v=DV), AX.X, ALU.add)\
                           .then_inc(s_pow, 1)
                        dve.wait_ge(s_pow, c + 1)
                        dve.tensor_scalar(var[:, n], power[:, n], 1.0 / DV, 1e-5, ALU.mult, ALU.add).then_inc(s_var, 1)
                        dve.wait_ge(s_rstd, c + 1)
                        dve.tensor_tensor(on[:, n].rearrange("p (a v) -> p a v", v=DV),
                                          o[:, n].rearrange("p (a v) -> p a v", v=DV), across(rstd[:, n], DV), ALU.mult)\
                           .then_inc(s_on, 1)

                    def result(n):
                        c = b * 2 + n
                        dve.wait_ge(s_y, c + 1)
                        x = g.x_tok[:, bass.ds(c * 4, 4), :]
                        dve.tensor_tensor(x, p_y[:].rearrange("p (i d) -> p i d", i=4), x, ALU.add).then_inc(s_res, 1)

                    dve.memset(state[:], 0.0).then_inc(s_state, 1)
                    dve.wait_ge(s_state, b * STEPS + 1)
                    for n in range(2):
                        values(n, 0)
                        if n:
                            norm(0)
                        for pair in range(2):
                            mask(n, pair)
                            values(n, 2 * pair + 1)
                            update_state(n, 2 * pair)
                            if pair == 0:
                                values(n, 2)
                            update_state(n, 2 * pair + 1)
                            if n == 1 and pair == 0:
                                result(0)
                    norm(1)
                    result(1)


DEPTH, LOCAL_HEADS, LOCAL_DH, WINDOW = 6, 16, 64, 32
INNER = LOCAL_HEADS * LOCAL_DH
PAIRS = LOCAL_HEADS // 2
KEYS = P + WINDOW
HALVES = 6
HH = LOCAL_HEADS // 2
ORDER = (2, 3, 0, 1)


def mirror(nc, g):
    with Phase(nc, "mirror") as ph:
        zero = ph.sb("zero", [BATCH, D])
        s_zero, s_st = ph.sem("zero"), ph.sem("st")
        with nc.Block() as block:
            @block.gpsimd
            def _(pool):
                pool.memset(zero[:], 0.0).then_inc(s_zero, 1)

            @block.vector
            def _(dve):
                dve.tensor_copy(g.xT[:], g.x_tok[:].rearrange("p t d -> p (t d)"))

            @block.sync
            def _(sp):
                for b in range(BATCH):
                    sp.dma_start(g.mirrors[0][b * (SEQ + 1) + 1:(b + 1) * (SEQ + 1), :].rearrange("(j p) d -> p j d", p=P),
                                 g.x_tok[:, b * TB:(b + 1) * TB, :]).then_inc(s_st, 16)
                sp.wait_ge(s_zero, 1)
                for m in g.mirrors:
                    sp.dma_start(m[0:BATCH * (SEQ + 1)].rearrange("(n s) d -> n s d", s=SEQ + 1)[:, 0, :], zero[:]).then_inc(s_st, 16)
                sp.wait_ge(s_st, 16 * (BATCH + 2))
                ph.clear_before(sp)


def local_attention(nc, g, layer):
    source, target = g.mirrors
    with Phase(nc, "loc") as ph:
        wqkv = ph.sb("wqkv", [P, 3 * INNER])
        wo = ph.sb("wo", [P, PAIRS, D])
        mask16 = ph.sb("mask16", [P, 3, 2 * KEYS], BF16)
        ident16 = ph.sb("ident16", [P, P], BF16)
        maskin = ph.sb("maskin", [P, 2, 2 * KEYS])
        table = ph.sb("table", [P, 4, TB, LOCAL_DH])
        scales = ph.sb("scales", [P, 4, LOCAL_DH])
        slot = ph.sb("slot", [P, 2, D])
        sT = ph.sb("sT", [P, P])
        rot = ph.sb("rot", [P, 4, HH, LOCAL_DH])
        part = ph.sb("part", [P, 4, HH, LOCAL_DH])
        square = ph.sb("square", [P, 4, HH, LOCAL_DH])
        power = ph.sb("power", [P, 2, 2 * LOCAL_HEADS])
        floor_ = ph.sb("floor", [P, 2, 2 * LOCAL_HEADS])
        rnorm = ph.sb("rnorm", [P, 2, 2 * LOCAL_HEADS])
        kn = ph.sb("kn", [P, LOCAL_HEADS, LOCAL_DH])
        qT = ph.sb("qT", [P, PAIRS, P])
        kT = ph.sb("kT", [P, 2, PAIRS, 2, KEYS])
        v = ph.sb("v", [P, 2, INNER])
        v_before = ph.sb("v_before", [P, 2, INNER])
        top = ph.sb("top", [P, PAIRS, 2])
        ntop = ph.sb("ntop", [P, PAIRS, 2])
        total = ph.sb("total", [P, PAIRS, 2])
        share = ph.sb("share", [P, PAIRS, 2])
        probs = ph.sb("probs", [P, 2, 2, KEYS])
        normed = ph.sb("normed", [P, 2, 2, KEYS])
        pT = ph.sb("pT", [P, 2, 2 * KEYS])
        oT = ph.sb("oT", [P, PAIRS, P])
        p_t = ph.ps("t", [P, CH])
        p_w = [ph.ps(f"w{i}", [P, CH]) for i in range(2)]
        p_s = [ph.ps(f"s{i}", [P, CH]) for i in range(2)]
        p_p = ph.ps("p", [P, CH])
        p_o = [ph.ps(f"o{i}", [P, CH]) for i in range(2)]
        s_in, s_const, s_clear, s_tab = ph.sem("in"), ph.sem("const"), ph.sem("clear"), ph.sem("tab")
        s_slot, s_xt, s_xtc = ph.two("slot"), ph.sem("xt"), ph.sem("xtc")
        s_w, s_mul, s_free, s_power, s_add, s_floor, s_pow, s_kn = (
            ph.sem("w"), ph.sem("mul"), ph.two("free"), ph.sem("power"), ph.sem("add"), ph.sem("floor"),
            ph.sem("pow"), ph.sem("kn"))
        kept = ph.sb("kept", [P, 3, WINDOW])
        s_kept = ph.sem("kept_set")
        s_b, s_ba, s_bd, s_kb, s_vb = (ph.sem(n) for n in ("b", "ba", "bd", "kb", "vb"))
        s_s, s_top, s_ntop, s_exp, s_share, s_norm, s_turn, s_pt, s_pv, s_tile = (
            ph.sem(n) for n in ("s", "top", "ntop", "exp", "share", "norm", "turn", "pt", "pv", "tile"))
        s_oc, s_y, s_res, s_st = (ph.sem(n) for n in ("oc", "y", "res", "st"))
        INS = 5

        def first_row(t):
            return t * P + (t >> 3) + 1

        def loop(eng, prologue, body):
            prologue()
            with eng.Fori(0, NT // 2 - 1) as it:
                for u in range(2):
                    body(it * 2 + u, u, True, True)
            body(NT - 2, 0, True, False)
            body(NT - 1, 1, False, False)

        with nc.Block() as block:
            @block.sync
            def _(sp):
                def load(t, s):
                    row = first_row(t)
                    sp.dma_start(slot[:, s, 0:LOCAL_DH], source[bass.ds(row, P), 0:LOCAL_DH])\
                      .then_inc(s_slot[s], 16)
                    sp.dma_start(slot[:, s, LOCAL_DH:D], source[bass.ds(row - 1, P), LOCAL_DH:D])\
                      .then_inc(s_slot[s], 16)

                def body(t, s, more, ahead=True):
                    if more:
                        for n in range(2):
                            sp.wait_ge(s_free[n], t * 3 + 3)
                        sp.wait_ge(s_tile, t)
                        sp.dma_start(v_before[P - WINDOW:P, 1 - s, :], v[P - WINDOW:P, s, :]).then_inc(s_vb, 16)
                    if ahead:
                        sp.wait_ge(s_xt, t + 1)
                        load(t + 2, s)
                    sp.wait_ge(s_res, t + 1)
                    row = first_row(t)
                    sp.dma_start(target[bass.ds(row, P), :],
                                 g.x_tok[:, bass.ds(t, 1), :].rearrange("p a d -> p (a d)")).then_inc(s_st, 16)

                sp.dma_start(wqkv[:], g.dram["L3_ffn_Wqkv"][bass.ds(layer, 1), :, :].rearrange("a d n -> d (a n)")).then_inc(s_in, 16)
                load(0, 0)
                load(1, 1)
                sp.dma_start(table[:], g.dram["c_rotary"][:, :, :, :]).then_inc(s_in, 16)
                sp.dma_start(scales[:], g.dram["L3_ffn_scales"][bass.ds(layer, 1), :, :].rearrange("a k d -> (a k d)")
                             .partition_broadcast(P).rearrange("p (k d) -> p k d", d=LOCAL_DH)).then_inc(s_in, 16)
                sp.dma_start(maskin[:], g.dram["c_band32"][:, :, :]).then_inc(s_in, 16)
                sp.dma_start(wo[:], g.dram["L3_ffn_Wo"][bass.ds(layer, 1), :, :].rearrange("a (h p) n -> p (a h) n", p=P))\
                  .then_inc(s_in, 16)
                sp.wait_ge(s_clear, 2)
                with sp.Fori(0, NT // 2 - 1) as it:
                    for u in range(2):
                        body(it * 2 + u, u, True)
                body(NT - 2, 0, True, ahead=False)
                body(NT - 1, 1, False, ahead=False)
                sp.wait_ge(s_st, 16 * NT)
                ph.clear_before(sp)

            @block.tensor
            def _(pe):
                def shifted(t, s, k):
                    pe.wait_ge(s_slot[s], (k + 1) * 32)
                    pe.wait_ge(s_xtc, t)
                    if not isinstance(t, int) or t > 1:
                        pe.wait_ge(s_res, t - 2)
                    pe.transpose(p_t[:, 0:P], slot[:, s, :], g.ident[:]).then_inc(s_xt, 1)

                def project(t, n):
                    if n == 0:
                        pe.wait_ge(s_xtc, t + 1)
                    pe.wait_ge(s_free[n % 2], t * 3 + n // 2)
                    m = ORDER[n] if n < 4 else n
                    pe.matmul(p_w[n % 2][:], sT[:], wqkv[:, m * CH:(m + 1) * CH], start=True, stop=True).then_inc(s_w, 1)

                def turn_heads(t, which):
                    first = isinstance(t, int) and t == 0
                    for n in which:
                        bank = (p_o[0], p_s[0], p_s[1], p_p)[n]
                        if n == 0:
                            pe.wait_ge(s_add, t * 4 + 4)
                            if not first:
                                pe.wait_ge(s_oc, t * 2 - 1)
                        if n == 1 and not first:
                            pe.wait_ge(s_exp, t * PAIRS - 1)
                        if n == 2:
                            pe.wait_ge(s_exp, t * PAIRS)
                            pe.wait_ge(s_kn, t + 1)
                        if n == 3:
                            pe.wait_ge(s_pt, t * PAIRS)
                        for i in range(4):
                            pair = (n % 2) * 4 + i
                            if n < 2:
                                of = rot[:, pair // 4, 2 * (pair % 4):2 * (pair % 4) + 2, :]
                            else:
                                of = kn[:, 2 * pair:2 * pair + 2, :]
                            mm = pe.transpose(bank[:, i * P:(i + 1) * P], of.rearrange("p h d -> p (h d)"), g.ident[:])
                        mm.then_inc(s_b, 1)

                def scores(t, s, pair):
                    if pair == 0:
                        pe.wait_ge(s_ba, t * 3 + 3)
                        pe.wait_ge(s_bd, t * 2 + 2)
                        pe.wait_ge(s_kb, t)
                    if pair >= 2:
                        pe.wait_ge(s_exp, t * PAIRS + (pair - 1))
                    bank = p_s[pair % 2][:, 0:2 * KEYS]
                    later = ((t & 7) + 7) >> 3
                    pe.matmul(bank, ident16[:], mask16[:, bass.ds(later, 1), :] if not isinstance(t, int)
                              else mask16[:, later, :], start=True, stop=False)
                    pe.matmul(bank, qT[:, pair, :], kT[:, s, pair].rearrange("p a k -> p (a k)"), start=False, stop=True)\
                      .then_inc(s_s, 1)

                def turn(t, pair):
                    pe.wait_ge(s_norm, t * PAIRS + (pair + 1))
                    pe.wait_ge(s_pt, t * PAIRS + pair)
                    for h in range(2):
                        pe.transpose(p_p[:, h * P:(h + 1) * P], normed[:, pair % 2, h, 0:P], g.ident[:])
                        mm = pe.transpose(p_p[:, 2 * P + h * WINDOW:2 * P + (h + 1) * WINDOW],
                                          normed[0:WINDOW, pair % 2, h, WINDOW:KEYS], g.ident[0:WINDOW, 0:WINDOW])
                    mm.then_inc(s_turn, 1)

                def mix(t, s, pair):
                    pe.wait_ge(s_pt, t * PAIRS + (pair + 1))
                    if pair == 0:
                        pe.wait_ge(s_vb, t * 16)
                        for n in range(2):
                            pe.wait_ge(s_free[n], t * 3 + 3)
                    if pair % 4 == 0:
                        pe.wait_ge(s_oc, t * 2 + pair // 4)
                    for h in range(2):
                        rows = slice(h * LOCAL_DH, (h + 1) * LOCAL_DH)
                        cols = slice((2 * pair + h) * LOCAL_DH, (2 * pair + h + 1) * LOCAL_DH)
                        at = (pair % 4) * P
                        bank = p_o[pair // 4]
                        pe.matmul(bank[rows, at:at + P], v[:, s, cols], pT[:, pair % 2, h * P:(h + 1) * P],
                                  start=True, stop=False)
                        mm = pe.matmul(bank[rows, at:at + WINDOW], v_before[:, s, cols],
                                       pT[:, pair % 2, 2 * P + h * WINDOW:2 * P + (h + 1) * WINDOW], start=False, stop=True)
                    mm.then_inc(s_pv, 1)
                    if pair == PAIRS - 1:
                        pe.wait_ge(s_pv, (t + 1) * PAIRS)
                        pe.sem_inc(s_tile, 1)

                def out_project(t, more2):
                    pe.wait_ge(s_oc, t * 2 + 2)
                    pe.wait_ge(s_res, t)
                    if more2:
                        pe.wait_ge(s_xtc, t + 3)
                    for pair in range(PAIRS):
                        mm = pe.matmul(p_t[:, 0:D], oT[:, pair, :], wo[:, pair, :], start=(pair == 0), stop=(pair == PAIRS - 1))
                    mm.then_inc(s_y, 1)

                def prologue():
                    pe.wait_ge(s_in, 16 * INS)
                    shifted(0, 0, 0)
                    for n in range(HALVES):
                        project(0, n)
                    shifted(1, 1, 0)
                    turn_heads(0, (0, 1, 2, 3))
                    scores(0, 0, 0)
                    scores(0, 0, 1)

                def body(t, s, more, more2):
                    for pair in range(PAIRS):
                        if pair + 2 < PAIRS:
                            scores(t, s, pair + 2)
                        if more and pair < HALVES:
                            project(t + 1, pair)
                        turn(t, pair)
                        if more2 and pair == HALVES:
                            shifted(t + 2, s, (t >> 1) + 1)
                        if more and pair == PAIRS - 1:
                            turn_heads(t + 1, (0, 1, 2))
                        if pair:
                            mix(t, s, pair - 1)
                    mix(t, s, PAIRS - 1)
                    if more:
                        turn_heads(t + 1, (3,))
                        scores(t + 1, 1 - s, 0)
                        scores(t + 1, 1 - s, 1)
                    out_project(t, more2)

                pe.wait_ge(s_const, 2)
                pe.wait_ge(s_clear, 2)
                loop(pe, prologue, body)

            @block.vector
            def _(dve):
                def rotate(t, s, n):
                    dve.wait_ge(s_w, t * HALVES + (n + 1))
                    dve.wait_ge(s_b, t * 4)
                    dve.wait_ge(s_add, t * 4)
                    m, kind = ORDER[n], ORDER[n] // 2
                    cos, sin = (table[:, 2 * kind + i, bass.ds(t & 7, 1) if not isinstance(t, int) else slice(t & 7, (t & 7) + 1), :]
                                for i in range(2))
                    x = p_w[n % 2][:].rearrange("p (h d) -> p h d", d=LOCAL_DH)
                    dve.tensor_tensor(rot[:, m], x, cos.to_broadcast([P, HH, LOCAL_DH]), ALU.mult)
                    for half in range(2):
                        to, of = slice(half * 32, half * 32 + 32), slice(32 - half * 32, 64 - half * 32)
                        ins = dve.tensor_tensor(part[:, m, :, to], x[:, :, of],
                                                sin[:, :, to].to_broadcast([P, HH, LOCAL_DH // 2]), ALU.mult)
                    ins.then_inc(s_mul, 1)

                def norms(t, s, n):
                    dve.wait_ge(s_free[n % 2], t * 3 + (n // 2 + 1))
                    m = ORDER[n]
                    dve.tensor_reduce(power[:, s, m * HH:(m + 1) * HH], square[:, m], AX.X, ALU.add).then_inc(s_power, 1)
                    if n % 2:
                        dve.wait_ge(s_power, t * 4 + (n + 1))
                        half = slice((m - 1) * HH, (m + 1) * HH)
                        dve.tensor_scalar(floor_[:, s, half], power[:, s, half], 1e-24, None, ALU.max).then_inc(s_floor, 1)

                def scale_keys(t, s):
                    dve.wait_ge(s_add, t * 4 + 2)
                    dve.wait_ge(s_pow, t * 2 + 1)
                    dve.tensor_tensor(kn[:], rot[:, 2:4].rearrange("p a h d -> p (a h) d"),
                                      across(rnorm[:, s, LOCAL_HEADS:2 * LOCAL_HEADS], LOCAL_DH), ALU.mult).then_inc(s_kn, 1)

                def maximum(t, s, pair):
                    if pair == 0:
                        dve.wait_ge(s_pow, t * 2 + 2)
                    dve.wait_ge(s_s, t * PAIRS + (pair + 1))
                    dve.tensor_reduce(top[:, pair, :], p_s[pair % 2][:, 0:2 * KEYS].rearrange("p (a k) -> p a k", a=2),
                                      AX.X, ALU.max).then_inc(s_top, 1)
                    dve.wait_ge(s_top, t * PAIRS + (pair + 1))
                    dve.scalar_tensor_tensor(out=ntop[:, pair, :], in0=top[:, pair, :], scalar=-1.0,
                                             in1=rnorm[:, s, 2 * pair:2 * pair + 2], op0=ALU.mult, op1=ALU.mult)\
                       .then_inc(s_ntop, 1)

                def normalise(t, pair):
                    dve.wait_ge(s_exp, t * PAIRS + (pair + 1))
                    dve.reciprocal(share[:, pair, :], total[:, pair, :]).then_inc(s_share, 1)
                    dve.wait_ge(s_share, t * PAIRS + (pair + 1))
                    dve.wait_ge(s_turn, t * PAIRS + max(pair - 1, 0))
                    dve.tensor_tensor(normed[:, pair % 2], probs[:, pair % 2], across(share[:, pair, :], KEYS), ALU.mult)\
                       .then_inc(s_norm, 1)

                def second_heads(t, s):
                    for n in range(2):
                        dve.wait_ge(s_b, t * 4 + (3 + n))
                        dve.tensor_copy(kT[LOCAL_DH:P, s, 4 * n:4 * n + 4, 1, 0:P],
                                        (p_s[1], p_p)[n][LOCAL_DH:P, :].rearrange("p (a k) -> p a k", k=P)).then_inc(s_bd, 1)

                def result(t):
                    dve.wait_ge(s_y, t + 1)
                    x = g.x_tok[:, bass.ds(t, 1), :].rearrange("p a d -> p (a d)")
                    dve.tensor_tensor(x, p_t[:, 0:D], x, ALU.add).then_inc(s_res, 1)

                def prologue():
                    dve.wait_ge(s_in, 16 * INS)
                    dve.tensor_copy(mask16[:, 0:2, :], maskin[:]).then_inc(s_const, 1)
                    dve.tensor_copy(ident16[:], g.ident[:]).then_inc(s_const, 1)
                    for i in range(4):
                        dve.tensor_tensor(table[:, i], table[:, i], scales[:, i:i + 1, :].to_broadcast([P, TB, LOCAL_DH]), ALU.mult)\
                           .then_inc(s_tab, 1)
                    dve.wait_ge(s_tab, 4)
                    for n in range(4):
                        rotate(0, 0, n)
                        norms(0, 0, n)
                    scale_keys(0, 0)
                    second_heads(0, 0)
                    maximum(0, 0, 0)
                    maximum(0, 0, 1)

                def body(t, s, more, more2):
                    for pair in range(PAIRS):
                        if 1 <= pair < PAIRS - 1:
                            maximum(t, s, pair + 1)
                        normalise(t, pair)
                        if pair == 0 and not (isinstance(t, int) and t == 0):
                            result(t - 1)
                        if more and pair < 4:
                            rotate(t + 1, 1 - s, pair)
                        if more and 1 <= pair <= 4:
                            norms(t + 1, 1 - s, pair - 1)
                        if more and pair == PAIRS - 3:
                            scale_keys(t + 1, 1 - s)
                    if more:
                        second_heads(t + 1, 1 - s)
                        maximum(t + 1, 1 - s, 0)
                        maximum(t + 1, 1 - s, 1)

                prologue()
                body(0, 0, True, True)
                body(1, 1, True, True)
                with dve.Fori(0, NT // 2 - 2) as it:
                    for u in range(2):
                        body(it * 2 + (2 + u), u, True, True)
                body(NT - 2, 0, True, False)
                body(NT - 1, 1, False, False)
                result(NT - 1)

            @block.scalar
            def _(act):
                def shifted(t):
                    act.wait_ge(s_xt, t + 1)
                    act.wait_ge(s_w, t * HALVES)
                    act.activation(sT[:], p_t[:, 0:P], ACT.Copy).then_inc(s_xtc, 1)

                def squares(t, n):
                    act.wait_ge(s_mul, t * 4 + (n + 1))
                    act.wait_ge(s_power, t * 4)
                    act.activation(square[:, ORDER[n]].rearrange("p h d -> p (h d)"), p_w[n % 2][:], ACT.Square)\
                       .then_inc(s_free[n % 2], 1)

                def values(t, s, n):
                    act.wait_ge(s_w, t * HALVES + (n + 1))
                    act.activation(v[:, s, (n - 4) * CH:(n - 3) * CH], p_w[n % 2][:], ACT.Copy).then_inc(s_free[n % 2], 1)

                def exponentials(t, s, pair):
                    act.wait_ge(s_ntop, t * PAIRS + (pair + 1))
                    act.wait_ge(s_norm, t * PAIRS + max(pair - 1, 0))
                    for h in range(2):
                        head = 2 * pair + h
                        ins = act.activation(probs[:, pair % 2, h, :], p_s[pair % 2][:, h * KEYS:(h + 1) * KEYS], ACT.Exp,
                                             bias=ntop[:, pair, h:h + 1], scale=rnorm[:, s, head:head + 1],
                                             accum_out=total[:, pair, h:h + 1])
                    ins.then_inc(s_exp, 1)

                def turned(t, pair):
                    act.wait_ge(s_turn, t * PAIRS + (pair + 1))
                    act.wait_ge(s_pv, t * PAIRS + max(pair - 1, 0))
                    act.activation(pT[:, pair % 2, :], p_p[:, 0:2 * KEYS], ACT.Copy).then_inc(s_pt, 1)

                def mixed(t, n):
                    act.wait_ge(s_pv, t * PAIRS + 4 * (n + 1))
                    act.wait_ge(s_y, t)
                    act.activation(oT[:, 4 * n:4 * n + 4, :].rearrange("p a q -> p (a q)"), p_o[n][:], ACT.Copy)\
                       .then_inc(s_oc, 1)

                def prologue():
                    shifted(0)
                    for n in range(4):
                        squares(0, n)
                    values(0, 0, 4)
                    values(0, 0, 5)
                    shifted(1)
                    queries(0)
                    first_heads(0, 0, 0)
                    first_heads(0, 0, 1)
                    exponentials(0, 0, 0)

                def queries(t):
                    act.wait_ge(s_b, t * 4 + 1)
                    act.activation(qT[:, 0:4, :].rearrange("p a q -> p (a q)"), p_o[0][:], ACT.Copy).then_inc(s_ba, 1)
                    act.wait_ge(s_b, t * 4 + 2)
                    act.activation(qT[:, 4:8, :].rearrange("p a q -> p (a q)"), p_s[0][:], ACT.Copy)

                def first_heads(t, s, n):
                    act.wait_ge(s_b, t * 4 + (3 + n))
                    act.activation(kT[0:LOCAL_DH, s, 4 * n:4 * n + 4, 0, 0:P],
                                   (p_s[1], p_p)[n][0:LOCAL_DH, :].rearrange("p (a k) -> p a k", k=P), ACT.Copy)\
                       .then_inc(s_ba, 1)

                def body(t, s, more, more2):
                    for pair in range(PAIRS):
                        if pair + 1 < PAIRS:
                            exponentials(t, s, pair + 1)
                        if more and pair < 4:
                            squares(t + 1, pair)
                        turned(t, pair)
                        if more and 4 <= pair < HALVES:
                            act.wait_ge(s_tile, t)
                            act.wait_ge(s_vb, t * 16)
                            values(t + 1, 1 - s, pair)
                        if pair == 5:
                            mixed(t, 0)
                        if more2 and pair == HALVES:
                            shifted(t + 2)
                    if more:
                        queries(t + 1)
                        first_heads(t + 1, 1 - s, 0)
                    mixed(t, 1)
                    if more:
                        first_heads(t + 1, 1 - s, 1)
                        exponentials(t + 1, 1 - s, 0)

                act.wait_ge(s_clear, 2)
                loop(act, prologue, body)

            @block.gpsimd
            def _(pool):
                pool.memset(v_before[:], 0.0).then_inc(s_clear, 1)
                pool.memset(kT[:], 0.0).then_inc(s_clear, 1)
                pool.memset(kept[:, 0, :], 0.0).then_inc(s_kept, 1)
                pool.memset(kept[:, 1:3, :], 1.0).then_inc(s_kept, 1)
                pool.wait_ge(s_kept, 2)

                def add(t, n):
                    pool.wait_ge(s_mul, t * 4 + (n + 1))
                    m = ORDER[n]
                    pool.tensor_tensor(rot[:, m], rot[:, m], part[:, m], ALU.add).then_inc(s_add, 1)

                def reciprocal_norms(t, s, i):
                    kind = 1 - i
                    pool.wait_ge(s_floor, t * 2 + (i + 1))
                    half = slice(kind * LOCAL_HEADS, (kind + 1) * LOCAL_HEADS)
                    pool.tensor_tensor(rnorm[:, s, half], floor_[:, s, half], g.minus_half[:, 0:LOCAL_HEADS], ALU.pow).then_inc(s_pow, 1)

                def prologue():
                    for n in range(4):
                        add(0, n)
                        if n % 2:
                            reciprocal_norms(0, 0, n // 2)

                def body(t, s, more, more2):
                    if more:
                        pool.wait_ge(s_ba, t * 3 + 3)
                        pool.wait_ge(s_bd, t * 2 + 2)
                        later = (((t + 1) & 7) + 7) >> 3
                        keep = kept[:, later:later + 1, :] if isinstance(t, int) else kept[:, bass.ds(later, 1), :]
                        pool.tensor_tensor(kT[:, 1 - s, :, :, P:KEYS].rearrange("p a h k -> p (a h) k"),
                                           kT[:, s, :, :, P - WINDOW:P].rearrange("p a h k -> p (a h) k"),
                                           keep.to_broadcast([P, LOCAL_HEADS, WINDOW]), ALU.mult).then_inc(s_kb, 1)
                        pool.wait_ge(s_tile, t)
                        for n in range(4):
                            add(t + 1, n)
                            if n % 2:
                                reciprocal_norms(t + 1, 1 - s, n // 2)

                loop(pool, prologue, body)


FF = 341
FT = 3
TC = CH // P


def gated_ffn(nc, g, layer):
    target, source = g.mirrors
    with Phase(nc, "gff") as ph:
        w1 = ph.sb("w1", [P, 2 * FT * P])
        b1 = ph.sb("b1", [P, 2 * FT])
        gain = ph.sb("gain", [P, 2])
        w2 = ph.sb("w2", [P, FT, D])
        b2 = ph.sb("b2", [1, D])
        slot = ph.sb("slot", [P, 2, TC, D])
        total = ph.sb("total", [P, 2, TC])
        mean = ph.sb("mean", [P, 2, TC])
        power = ph.sb("power", [P, 2, TC])
        variance = ph.sb("variance", [P, 2, TC])
        rstd = ph.sb("rstd", [P, 2, TC])
        centred = ph.sb("centred", [P, 2, TC, D])
        squares = ph.sb("squares", [P, 2, TC, D])
        normed = ph.sb("normed", [P, 2, TC, D])
        xn = ph.sb("xn", [P, 2, CH])
        gate = ph.sb("gate", [P, 2, FT, CH])
        h = ph.sb("h", [P, 2, FT, CH])
        p_t = ph.ps("t", [P, CH])
        p_g = [ph.ps(f"g{i}", [P, CH]) for i in range(2)]
        p_a = [ph.ps(f"a{i}", [P, CH]) for i in range(2)]
        p_y = [ph.ps(f"y{i}", [P, CH]) for i in range(2)]
        s_in, s_slot, s_st = ph.sem("in"), ph.two("slot"), ph.sem("st")
        s_total, s_mean, s_cent, s_sq, s_power, s_var, s_rstd, s_norm = (
            ph.sem(n) for n in ("total", "mean", "cent", "sq", "power", "var", "rstd", "norm"))
        s_t, s_xn, s_g, s_gelu, s_a, s_h, s_y, s_res = (
            ph.sem(n) for n in ("t", "xn", "g", "gelu", "a", "h", "y", "res"))
        INS = 5

        def chunks(eng, prologue, body):
            prologue()
            with eng.Fori(0, NCH // 2 - 1) as it:
                for u in range(2):
                    body(it * 2 + u, u, True)
            body(NCH - 2, 0, True)
            body(NCH - 1, 1, False)

        def first_row(c):
            return c * CH + (c >> 1) + 1

        with nc.Block() as block:
            @block.sync
            def _(sp):
                def load(c, s):
                    row = first_row(c)
                    sp.dma_start(slot[:, s, :, 0:D // 2],
                                 source[bass.ds(row, CH), 0:D // 2].rearrange("(j p) d -> p j d", p=P)).then_inc(s_slot[s], 16)
                    sp.dma_start(slot[:, s, :, D // 2:D],
                                 source[bass.ds(row - 1, CH), D // 2:D].rearrange("(j p) d -> p j d", p=P)).then_inc(s_slot[s], 16)

                def body(c, s, more, ahead=True):
                    if ahead:
                        sp.wait_ge(s_cent, c + 1)
                        load(c + 2, s)
                    sp.wait_ge(s_res, c + 1)
                    sp.dma_start(target[bass.ds(first_row(c), CH), :].rearrange("(j p) d -> p j d", p=P),
                                 g.x_tok[:, bass.ds(c * TC, TC), :]).then_inc(s_st, 16)

                load(0, 0)
                load(1, 1)
                sp.dma_start(gain[:], g.dram["L3_ffn_gain"][bass.ds(layer, 1), :, :].rearrange("a p n -> (a p) n")).then_inc(s_in, 16)
                sp.dma_start(w1[:], g.dram["L3_ffn_W1p"][bass.ds(layer, 1), :, :].rearrange("a p n -> (a p) n")).then_inc(s_in, 16)
                sp.dma_start(b1[:], g.dram["L3_ffn_b1T"][bass.ds(layer, 1), :, :].rearrange("a p n -> (a p) n")).then_inc(s_in, 16)
                sp.dma_start(w2[:], g.dram["L3_ffn_W2p"][bass.ds(layer, 1), :, :].rearrange("a (f p) n -> p (a f) n", p=P))\
                  .then_inc(s_in, 16)
                sp.dma_start(b2[:], g.dram["L3_ffn_b2"][bass.ds(layer, 1), :]).then_inc(s_in, 16)
                with sp.Fori(0, NCH // 2 - 1) as it:
                    for u in range(2):
                        body(it * 2 + u, u, True)
                body(NCH - 2, 0, True, ahead=False)
                body(NCH - 1, 1, False, ahead=False)
                sp.wait_ge(s_st, 16 * NCH)
                ph.clear_before(sp)

            @block.vector
            def _(dve):
                def centre(c, s, k):
                    dve.wait_ge(s_slot[s], k * 32 + 32)
                    dve.tensor_reduce(total[:, s], slot[:, s], AX.X, ALU.add).then_inc(s_total, 1)
                    dve.wait_ge(s_total, c + 1)
                    dve.tensor_scalar(mean[:, s], total[:, s], 1.0 / D, None, ALU.mult).then_inc(s_mean, 1)
                    dve.wait_ge(s_mean, c + 1)
                    dve.tensor_tensor(centred[:, s], slot[:, s], across(mean[:, s], D), ALU.subtract).then_inc(s_cent, 1)

                def powers(c, s):
                    dve.wait_ge(s_sq, c + 1)
                    dve.tensor_reduce(power[:, s], squares[:, s], AX.X, ALU.add).then_inc(s_power, 1)
                    dve.wait_ge(s_power, c + 1)
                    dve.tensor_scalar(variance[:, s], power[:, s], 1.0 / D, 1e-5, ALU.mult, ALU.add).then_inc(s_var, 1)

                def normalise(c, s, k):
                    dve.wait_ge(s_rstd, c + 1)
                    if k is not None:
                        dve.wait_ge(s_t, c - 1)
                    dve.tensor_tensor(normed[:, s], centred[:, s], across(rstd[:, s], D), ALU.mult).then_inc(s_norm, 1)

                def product(c, s, f):
                    dve.wait_ge(s_a, c * FT + (f + 1))
                    dve.wait_ge(s_gelu, c * FT + (f + 1))
                    dve.scalar_tensor_tensor(out=h[:, s, f, :], in0=p_a[f % 2][:], scalar=b1[:, f:f + 1], in1=gate[:, s, f, :],
                                             op0=ALU.add, op1=ALU.mult).then_inc(s_h, 1)

                def result(c, s):
                    dve.wait_ge(s_y, c + 1)
                    x = g.x_tok[:, bass.ds(c * TC, TC), :]
                    dve.tensor_tensor(x, p_y[s][:].rearrange("p (j d) -> p j d", d=D), x, ALU.add).then_inc(s_res, 1)

                def prologue():
                    dve.wait_ge(s_in, 16 * INS)
                    centre(0, 0, 0)
                    powers(0, 0)
                    normalise(0, 0, None)

                def body(c, s, more):
                    if more:
                        centre(c + 1, 1 - s, (c + 1) >> 1)
                    product(c, s, 0)
                    if more:
                        powers(c + 1, 1 - s)
                    product(c, s, 1)
                    product(c, s, 2)
                    if more:
                        normalise(c + 1, 1 - s, c)
                    result(c, s)

                chunks(dve, prologue, body)

            @block.gpsimd
            def _(pool):
                def roots(c, s):
                    pool.wait_ge(s_var, c + 1)
                    pool.tensor_tensor(rstd[:, s], variance[:, s], g.minus_half[:, 0:TC], ALU.pow).then_inc(s_rstd, 1)

                def body(c, s, more):
                    if more:
                        roots(c + 1, 1 - s)

                chunks(pool, lambda: roots(0, 0), body)

            @block.scalar
            def _(act):
                def square(c, s):
                    act.wait_ge(s_cent, c + 1)
                    act.activation(squares[:, s], centred[:, s], ACT.Square).then_inc(s_sq, 1)

                def turned(c, s, k):
                    act.wait_ge(s_t, c + 1)
                    if k is not None:
                        act.wait_ge(s_a, (c - 1) * FT)
                    act.activation(xn[:, s, :], p_t[:], ACT.Identity, bias=gain[:, 1:2], scale=gain[:, 0:1]).then_inc(s_xn, 1)

                def gates(c, s, f):
                    act.wait_ge(s_g, c * FT + (f + 1))
                    act.activation(gate[:, s, f, :], p_g[f % 2][:], ACT.Gelu, bias=b1[:, FT + f:FT + f + 1]).then_inc(s_gelu, 1)

                def prologue():
                    square(0, 0)
                    turned(0, 0, None)

                def body(c, s, more):
                    gates(c, s, 0)
                    if more:
                        square(c + 1, 1 - s)
                    gates(c, s, 1)
                    gates(c, s, 2)
                    if more:
                        turned(c + 1, 1 - s, c)

                act.wait_ge(s_in, 16 * INS)
                chunks(act, prologue, body)

            @block.tensor
            def _(pe):
                def turn(c, s):
                    pe.wait_ge(s_norm, c + 1)
                    pe.wait_ge(s_xn, c)
                    for j in range(TC):
                        mm = pe.transpose(p_t[:, j * P:(j + 1) * P], normed[:, s, j, :], g.ident[:])
                    mm.then_inc(s_t, 1)

                def hidden(c, s, f):
                    if f >= 2:
                        pe.wait_ge(s_h, c * FT + (f - 1))
                    else:
                        pe.wait_ge(s_h, c * FT)
                    for bank, n, sem in ((p_g, FT + f, s_g), (p_a, f, s_a)):
                        pe.matmul(bank[f % 2][:], w1[:, n * P:(n + 1) * P], xn[:, s, :], start=True, stop=True).then_inc(sem, 1)

                def output(c, s):
                    pe.wait_ge(s_h, c * FT + FT)
                    pe.wait_ge(s_res, c)
                    for j in range(TC):
                        at = p_y[s][:, j * D:(j + 1) * D]
                        for f in range(FT):
                            pe.matmul(at, h[:, s, f, j * P:(j + 1) * P], w2[:, f, :], start=(f == 0), stop=False)
                        mm = pe.matmul(at, g.ones[0:1, :], b2[:], start=False, stop=True)
                    mm.then_inc(s_y, 1)

                def body(c, s, more):
                    pe.wait_ge(s_xn, c + 1)
                    for f in range(FT):
                        hidden(c, s, f)
                    if more:
                        turn(c + 1, 1 - s)
                    output(c, s)

                pe.wait_ge(s_in, 16 * INS)
                chunks(pe, lambda: turn(0, 0), body)


def add_kept(nc, g):
    with Phase(nc, "kept") as ph:
        with nc.Block() as block:
            @block.sync
            def _(sp):
                ph.clear_before(sp)

            @block.vector
            def _(dve):
                dve.tensor_tensor(g.x_tok[:].rearrange("p t d -> p (t d)"), g.x_tok[:].rearrange("p t d -> p (t d)"), g.xT[:],
                                  ALU.add)


def local_transformer(nc, g):
    rows = BATCH * (SEQ + 1) + CH
    g.mirrors = [nc.dram_tensor(f"mirror{i}", (rows, D), F32, kind="Internal").ap() for i in range(2)]
    mirror(nc, g)
    clear_now(nc)
    with nc.Fori(0, DEPTH) as layer:
        local_attention(nc, g, layer)
        gated_ffn(nc, g, layer)
        clear_now(nc)
    add_kept(nc, g)


def transformer(nc, dram):
    g = Shared()
    g.dram = dram
    with ExitStack() as ctx:
        def sb(name, shape):
            return ctx.enter_context(nc.sbuf_tensor(name, shape, F32))

        g.x_tok = sb("x_tok", [P, NT, D])
        g.xT = sb("xT", [P, NT * P])
        g.ident = sb("ident", [P, P])
        g.ones = sb("ones", [P, P])
        g.minus_half = sb("minus_half", [P, 32])
        load_constants(nc, g)
        biased_attention(nc, g)
        layer_norm(nc, g)
        binary_ffn(nc, g)
        layer_norm(nc, g)
        linear_attention(nc, g)
        layer_norm(nc, g)
        with nc.sbuf_tensor("gates", [P, NT, EXPERTS], F32) as g.gates:
            route(nc, g)
            experts(nc, g)
        layer_norm(nc, g)
        multilevel_attention(nc, g)
        layer_norm(nc, g)
        lilora(nc, g)
        layer_norm(nc, g)
        hedgehog(nc, g)
        layer_norm(nc, g, transposed=False)
        local_transformer(nc, g)
        layer_norm(nc, g, transposed=False)
        store_output(nc, g)
        clear_now(nc)


def spread(w):
    out = np.zeros(w.shape[:-1] + (16, 32), np.float32)
    out[..., :8] = w.reshape(w.shape[:-1] + (16, 8))
    return out.reshape(w.shape[:-1] + (512,))


def feature_map(w):
    out = np.zeros((8, 16, 2, 4, 2, 16), np.float32)
    for head in range(8):
        out[head, :, head // 4, head % 4] = w.T[:, None, :]
    return out.reshape(P, 256)


def rotary_tables():
    f32 = np.float32
    half = np.arange(0, 64, 2).astype(f32)
    inverse = (f32(1) / np.power(f32(10000), half / f32(64))).astype(f32)
    t = np.arange(SEQ).astype(f32)
    angle = (t[:, None] * inverse[None]).astype(f32)
    angle = np.concatenate([angle, angle], -1).astype(np.float64)
    base = ((half + f32(0.4 * 64)) / f32(1.4 * 64)).astype(f32)
    scale = base[None].astype(np.float64) ** ((t - SEQ // 2) / 16)[:, None]
    scale = np.concatenate([scale, scale], -1)
    sign = np.where(np.arange(64) < 32, -1, 1)
    cos, sin = np.cos(angle), np.sin(angle) * sign
    tables = np.stack([8 * cos * scale, 8 * sin * scale, cos / scale, sin / scale]).astype(f32)
    return tables.reshape(4, TB, P, 64).transpose(2, 0, 1, 3)


def mask_constants():
    f32 = np.float32
    at = np.arange(P)
    q, k = at[:, None], at[None]
    c = {"c_ident": np.eye(P, dtype=f32)}
    c["c_same_head8"] = (q // 8 == k // 8).astype(f32)
    c["c_sign"] = np.where(at % 32 < 16, 1, -1).astype(f32)[:, None]
    c["c_causal"] = (q <= k).astype(f32)
    c["c_own_head"] = (q // 32 == np.arange(64)[None] // 16).astype(f32)
    sizes = np.repeat([1, 8, 16, 32, 64], [64, 16, 8, 8, 8]).astype(f32)
    there = np.ones((TB, 104), f32)
    there[0, :72] = there[0, 80:] = there[:2, 88:96] = there[:4, 96:] = 0
    c["c_there"] = np.concatenate([np.ones((TB, P), f32), there], 1).reshape(1, -1)
    c["c_there_sum"] = (there * sizes).reshape(1, -1)
    c["c_mean_of"] = np.tile(1 / sizes, (P, 1)).astype(f32)
    c["c_count"] = sizes[:, None]
    before = np.arange(64)[None] - 64
    first_level = np.concatenate([np.repeat(q < 64, 8, 1), np.repeat(q >= 64, 8, 1)], 1)
    seen = np.concatenate([(k <= q) & (k >= q - 63), before >= q - 63, first_level, np.ones((P, 24), bool)], 1)
    c["c_band64"] = np.tile(np.where(seen, 0, NEG), (1, 2)).astype(f32)
    before = np.arange(32)[None] - 32
    own, earlier = (k <= q) & (k >= q - 32), before >= q - 32
    seen = np.stack([np.concatenate([own, earlier & False], 1), np.concatenate([own, earlier], 1)], 1)
    c["c_band32"] = np.tile(np.where(seen, 0, NEG), (1, 1, 2)).astype(f32)
    c["c_rotary"] = rotary_tables()
    return c


def laid_out(i):
    a = dict(i)
    a.update(mask_constants())
    a["L0_attn_xT"] = i["L0_attn_x"].reshape(BATCH * SEQ, D).T
    a["L0_attn_wT"] = np.stack([i["L0_attn_W" + n].T for n in "qkv"], 1)
    a["L0_attn_bqk"] = np.stack([i["L0_attn_bq"], i["L0_attn_bk"]], 1)
    a["L0_attn_bv_row"] = i["L0_attn_bv"][None]
    a["L0_attn_bo_row"] = i["L0_attn_bo"][None]
    a["L0_attn_woT"] = i["L0_attn_Wo"].T
    distance = np.arange(SEQ + TB - 1)[None] - (TB - 1) - TB * np.arange(P)[:, None]
    a["L0_attn_bias"] = i["L0_attn_time_bias"][0, 0][np.clip(distance + 250, 0, 499)]
    a["L0_ffn_b1T"] = i["L0_ffn_b1"].reshape(4, P).T
    w, b = i["L2_attn_W_attn"], i["L2_attn_b_attn"]
    a["L2_attn_wq"], a["L2_attn_wk"], a["L2_attn_wv"] = spread(w[:, :D]), spread(w[:, D:2 * D]), w[:, 2 * D:]
    a["L2_attn_bq"] = spread(b[:D]).reshape(4, P).T
    a["L2_attn_bk_row"] = spread(b[D:2 * D])[None]
    a["L2_attn_bv_row"] = b[2 * D:][None]
    a["L2_attn_bproj"] = i["L2_attn_b_proj"][None]
    a["L2_ffn_down_T"] = i["L2_ffn_lora_down"].T
    a["L2_ffn_up_T"] = i["L2_ffn_lora_up"].T
    a["L2_ffn_up_auxT"] = i["L2_ffn_up_aux"].T
    a["L2_ffn_WT"] = i["L2_ffn_W"].T
    a["L3_attn_fq"], a["L3_attn_fk"] = feature_map(i["L3_attn_fmq_w"]), feature_map(i["L3_attn_fmk_w"])
    a["L3_attn_fb"] = np.stack([np.tile(i["L3_attn_fmq_b"], 8), np.tile(i["L3_attn_fmk_b"], 8)], 1)
    a["L3_attn_WvT"], a["L3_attn_WoT"] = i["L3_attn_Wv"].T, i["L3_attn_Wo"].T
    a["L3_attn_rms"] = np.tile(i["L3_attn_rms_w"], 8)[:, None]
    q, k = i["L3_ffn_q_scale"], i["L3_ffn_k_scale"]
    swapped = (np.arange(64) + 32) % 64
    a["L3_ffn_scales"] = np.stack([q, q[:, swapped], k, k[:, swapped]], 1)
    w, b = i["L3_ffn_W1"], i["L3_ffn_b1"]
    layers, pad = w.shape[0], 3 * P - 341
    zeros = np.zeros((layers, D, pad), np.float32)
    a["L3_ffn_W1p"] = np.concatenate([w[:, :, :341], zeros, w[:, :, 341:], zeros], 2)
    zeros = np.zeros((layers, pad), np.float32)
    a["L3_ffn_b1T"] = np.concatenate([b[:, :341], zeros, b[:, 341:], zeros], 1).reshape(layers, 6, P).transpose(0, 2, 1)
    a["L3_ffn_W2p"] = np.concatenate([i["L3_ffn_W2"], np.zeros((layers, pad, D), np.float32)], 1)
    a["L3_ffn_gain"] = np.stack([i["L3_ffn_ln_g"], i["L3_ffn_ln_b"]], 2)
    return a


ARRAYS = """
L0_attn_bias L0_attn_bo_row L0_attn_bqk L0_attn_bv_row L0_attn_et_gate L0_attn_is_gate L0_attn_wT
L0_attn_woT L0_attn_x L0_attn_xT L0_ffn_b1T L0_ffn_b2 L0_ffn_w1 L0_ffn_w2 L1_attn_Wk L1_attn_Wo
L1_attn_Wq L1_attn_Wv L1_ffn_gate_w L1_ffn_w1 L1_ffn_w2 L2_attn_W_proj L2_attn_bk_row L2_attn_bproj
L2_attn_bq L2_attn_bv_row L2_attn_wk L2_attn_wq L2_attn_wv L2_ffn_WT L2_ffn_b L2_ffn_down_T
L2_ffn_down_aux L2_ffn_up_T L2_ffn_up_auxT L3_attn_Wk L3_attn_WoT L3_attn_Wq L3_attn_WvT L3_attn_fb
L3_attn_fk L3_attn_fq L3_attn_rms L3_ffn_W1p L3_ffn_W2p L3_ffn_Wo L3_ffn_Wqkv L3_ffn_b1T L3_ffn_b2
L3_ffn_gain L3_ffn_scales c_band32 c_band64 c_causal c_count c_ident c_mean_of c_own_head c_rotary
c_same_head8 c_sign c_there c_there_sum
""".split()


def kernel(**inputs):
    import concourse.bacc as bacc
    from concourse.bass_utils import run_bass_kernel_spmd

    nc = bacc.Bacc("TRN2", target_bir_lowering=False, num_devices=1)
    laid = laid_out({name: np.asarray(value) for name, value in inputs.items()})
    arrays, dram = {}, {}
    for name in ARRAYS:
        arrays["in_" + name] = np.ascontiguousarray(laid[name])
        dram[name] = nc.dram_tensor("in_" + name, laid[name].shape, mybir.dt.from_np(laid[name].dtype),
                                    kind="ExternalInput").ap()
    dram["out"] = nc.dram_tensor("out", (BATCH, SEQ, D), F32, kind="ExternalOutput").ap()
    transformer(nc, dram)
    return run_bass_kernel_spmd(nc, [arrays], core_ids=[0]).results[0]["out"]
```
